# Optimizing a Trainium2 kernel written in Bass

```python
import numpy as np
import jax
import jax.numpy as jnp

def _softmax(x, axis=-1):
    return jax.nn.softmax(x, axis=axis)

def _gelu(x):
    return jax.nn.gelu(x, approximate=True)

def _silu(x):
    return jax.nn.silu(x)

def _sigmoid(x):
    return jax.nn.sigmoid(x)

def _layernorm(x, axis=-1, eps=1e-05):
    m = jnp.mean(x, axis=axis, keepdims=True)
    v = jnp.var(x, axis=axis, keepdims=True)
    return (x - m) / jnp.sqrt(v + eps)

def _scatter_add(tgt, idx, src, axis=0):
    return tgt.at[idx].add(src)

def _segment_sum(src, seg, n):
    return jax.ops.segment_sum(src, seg, n)
kernel_name = 'mk_adj_preln_d1_adj_r2_d7ee50'

def setup_inputs(seed: int=0):
    np.random.seed(seed)
    _w = jnp.asarray

    def _rec_inputs():
        import jax
        import jax.numpy as jnp
        _gk = jax.random.key(seed)
        x = -0.000929 + 1 * jax.random.normal(jax.random.fold_in(_gk, 1), (4096, 128), jnp.float32)
        _a = jax.random.bernoulli(jax.random.fold_in(_gk, 2), 0.000976562, (4096, 4096))
        _a = jnp.logical_or(_a, jnp.swapaxes(_a, -1, -2))
        _a = jnp.logical_or(_a, jnp.eye(4096, dtype=bool))
        adj = _a.astype(jnp.int32)
        return (x, adj)
    x, adj = _rec_inputs()

    def _L0_gnn_setup():
        import jax, jax.numpy as jnp
        import numpy as np
        N = 4096
        IN_F = 128
        OUT_F = 128
        ALPHA = 0.2
        NEG_INF = -9000000000000000.0
        key = jax.random.key(seed)
        k1, k2, k3, k4, k5 = jax.random.split(key, 5)
        mole_out = jax.random.normal(k1, (N, IN_F), dtype=jnp.float32)
        adj = jax.random.randint(k2, (N, N), 0, 2, dtype=jnp.int32)
        W = jax.random.normal(k3, (IN_F, OUT_F), dtype=jnp.float32) / np.sqrt(IN_F)
        a1 = jax.random.normal(k4, (OUT_F,), dtype=jnp.float32) / np.sqrt(2 * OUT_F)
        a2 = jax.random.normal(k5, (OUT_F,), dtype=jnp.float32) / np.sqrt(2 * OUT_F)
        return {'mole_out': mole_out, 'adj': adj, 'W': W, 'a1': a1, 'a2': a2}
    _L0_gnn_all = _L0_gnn_setup()
    _L0_gnn_in = {k: v for k, v in _L0_gnn_all.items() if k in ('W', 'a1', 'a2')}
    del _L0_gnn_all
    return {'x': x, 'adj': adj, 'L0_gnn_W': _L0_gnn_in['W'], 'L0_gnn_a1': _L0_gnn_in['a1'], 'L0_gnn_a2': _L0_gnn_in['a2']}

def reference(x, adj, L0_gnn_W, L0_gnn_a1, L0_gnn_a2):
    import jax
    import jax.numpy as jnp

    def _L0_gnn_ref(mole_out, adj, W, a1, a2):
        import jax, jax.numpy as jnp
        import numpy as np
        N = 4096
        IN_F = 128
        OUT_F = 128
        ALPHA = 0.2
        NEG_INF = -9000000000000000.0
        Wh = mole_out @ W
        s1 = Wh @ a1
        s2 = Wh @ a2
        e = jax.nn.leaky_relu(s1[:, None] + s2[None, :], negative_slope=ALPHA)
        att = jnp.where(adj > 0, e, NEG_INF)
        att = jax.nn.softmax(att, axis=1)
        h_prime = att @ Wh
        return jax.nn.elu(h_prime)
    h = jnp.maximum(_layernorm(x, axis=-1), 0.0)
    x = x + _L0_gnn_ref(h, adj, L0_gnn_W, L0_gnn_a1, L0_gnn_a2)
    return x

_drawn_inputs = setup_inputs


def setup_inputs(seed=0):
    import zlib

    import numpy as np

    out = dict(_drawn_inputs(seed))
    spreads = {}
    factors = {}
    for name, (base, spread) in spreads.items():
        noise = np.random.default_rng([zlib.crc32(name.encode()), seed]).standard_normal(out[name].shape)
        drawn = base * np.exp(spread * noise) if base else spread * noise
        out[name] = jnp.asarray(drawn.astype(out[name].dtype))
    for name, factor in factors.items():
        out[name] = (out[name] * factor).astype(out[name].dtype)
    return out
```

```python
import concourse.bass as bass
from concourse import mybir
from contextlib import ExitStack


def build(nc, x, adj, W, a1, a2, out):
    f32, i32 = mybir.dt.float32, mybir.dt.int32
    f16, u8, i8, fp8 = mybir.dt.float16, mybir.dt.uint8, mybir.dt.int8, mybir.dt.float8e4
    ALU = mybir.AluOpType
    ACT = mybir.ActivationFunctionType
    AX = mybir.AxisListType

    N, D = x.shape
    P = 128
    B = 4
    G = N // (P * B)
    S = G * B
    GC = P * B
    H = 2
    HC = N // H
    HG = G // H
    HS = S // H
    GH = B * H
    C = D + 1
    TILES = B
    ALPHA = 0.2
    NEG_INF = -9000000000000000.0
    EPS = 1e-5
    SPREAD = 8.0
    EDGE = 8
    DEN_SCALE = 2.0 ** 14
    WH_SCALE = 2.0 ** 11
    SSQ_MIN, SSQ_MAX = 1e-30, 1e30

    x_v = x.rearrange("(w p b) d -> p w (b d)", p=P, b=B)
    out_v = out.rearrange("(w p b) d -> w p (b d)", p=P, b=B)
    adj_v = adj.rearrange("(w p b) j -> w b p j", p=P, b=B)

    ctx = ExitStack()
    with ctx:
        def sb(name, shape, dt):
            return ctx.enter_context(nc.sbuf_tensor(name, shape, dt))

        def sem(name):
            return ctx.enter_context(nc.semaphore(name))

        x_sb = sb("x_sb", [P, S, D], f32)
        T_mem = sb("T_mem", [P, 2 * N], f32)
        hT = T_mem[:, 0:N].rearrange("p (s q) -> p s q", q=P)
        T8 = T_mem[:, :].bitcast(i8).rearrange("p (r w i b) -> p r w i b", r=2, w=G, b=B)
        T32 = T_mem[:, :].bitcast(i32).rearrange("p (r w i) -> p r w i", r=2, w=G)
        s1row = sb("s1row", [P, N], f32)
        WhM = sb("WhM", [P, S * C], f32)
        Wh = WhM[:, :].rearrange("p (s c) -> p s c", c=C)
        partB = WhM[:, 0:B * 2 * C].rearrange("p (s c) -> p s c", s=B)
        both = WhM[:, B * 2 * C:2 * B * 2 * C].rearrange("p (s c) -> p s c", s=B)
        num = WhM[:, 4 * B * C:5 * B * C].rearrange("p (s c) -> p s c", s=B)
        hp = WhM[:, 5 * B * C:5 * B * C + B * D].rearrange("p (s d) -> p s d", s=B)
        YA = sb("YA", [P, S, 2 * C], f16)
        YB = sb("YB", [P, S, 2 * C], f16)
        adj_sb = sb("adj_sb", [P, TILES, N], i32)
        V = sb("V", [P, H, HC], u8)
        AT = sb("AT", [P, H, HG, P], i32)
        BT = sb("BT", [P, H, HG, P], i32)
        scratch = sb("scratch", [P, 4 * B * C], f32)
        h_sb = scratch[:, 0:2 * GC].rearrange("p (r s d) -> p r s d", r=2, s=B)
        prodA = scratch[:, 0:2 * B * C].rearrange("p (r s c) -> p r s c", r=2, s=B)
        prodB = scratch[:, 2 * B * C:4 * B * C].rearrange("p (r s c) -> p r s c", r=2, s=B)
        eneg = scratch[:, 0:GC].rearrange("p (s d) -> p s d", s=B)
        res = scratch[:, GC:2 * GC].rearrange("p (s d) -> p s d", s=B)
        ident = sb("ident", [P, P], f32)
        ones = sb("ones", [P, P], f32)
        Wext = sb("Wext", [P, D + 2], f32)
        W_sb = sb("W_sb", [P, D], f32)
        wtmp = sb("wtmp", [P, D], f32)
        a_sb = sb("a_sb", [P, 2, D], f32)
        warep = sb("warep", [P, 2, P], f32)
        norm = sb("norm", [P, D], f32)
        unscale = sb("unscale", [P, D], f32)
        half = sb("half", [P, D], f32)
        minushalf = sb("minushalf", [P, S], f32)
        stats = sb("stats", [P, S, 6], f32)
        mv = sb("mv", [P, S, 2], f32)
        veps = sb("veps", [P, S], f32)
        rstd = sb("rstd", [P, S], f32)
        nmr = sb("nmr", [P, S], f32)
        hsum = sb("hsum", [P, G], f32)
        hsum1 = sb("hsum1", [P, 1], f32)
        hsumrep = sb("hsumrep", [P, P], f32)
        meanS = sb("meanS", [P, C], f32)
        s12 = sb("s12", [P, S, 2], f32)
        mm = sb("mm", [P, 2], f32)
        mmT = sb("mmT", [2, 1], f32)
        mmD = sb("mmD", [2, 2], f32)
        mmB = sb("mmB", [P, 2], f32)
        sF = sb("sF", [P, S], f32)
        u08 = sb("u08", [P, 2, S], f32)
        F1 = sb("F1", [P, S], f32)
        F2 = sb("F2", [P, S], f32)
        E = sb("E", [P, 2, S], f32)
        ssq_lim = sb("ssq_lim", [P, 2], f32)
        ok = sb("ok", [P, 4], f32)
        flag = sb("flag", [P, 1], i32)
        nonei = sb("nonei", [P, B], f32)
        rec = sb("rec", [P, B], f32)
        g_adj = adj_sb[:, 0, :]
        g_e = adj_sb[:, 1, :].bitcast(f32)
        g_m = adj_sb[:, 2, :].bitcast(f32)
        g_s2row = adj_sb[:, 3, :].bitcast(f32)
        g_PT = YA[:, :, :].rearrange("p s c -> p (s c)")[:, 0:4 * GC].bitcast(f32).rearrange(
            "p (r c) -> p r c", r=2)
        g_hp = scratch[:, 2 * GC:3 * GC].rearrange("p (s d) -> p s d", s=B)
        g_nmax = sb("g_nmax", [P, 1], f32)
        g_den = sb("g_den", [P, 1], f32)
        g_rec = sb("g_rec", [P, 1], f32)

        def bank(name):
            return ctx.enter_context(nc.psum_tensor(name, [P, 512], f32))

        TP = [bank("TP0"), bank("TP1")]
        PA = [bank("PA0"), bank("PA1")]
        PB = [bank("PB0"), bank("PB1")]
        PS12 = bank("PS12")
        PMISC = bank("PMISC")

        NX = 4
        x_loaded = [sem(f"x_loaded{i}") for i in range(NX)]
        w_loaded = sem("w_loaded")
        a_loaded = sem("a_loaded")
        adj_loaded = [sem(f"adj_loaded{i}") for i in range(TILES)]
        consts_set = sem("consts_set")
        ident_ready = sem("ident_ready")
        wsq_ready = sem("wsq_ready")
        ssq_done = sem("ssq_done")
        ssq_read = sem("ssq_read")
        norm_ready = sem("norm_ready")
        scale_step = sem("scale_step")
        wa_step = sem("wa_step")
        wext_ready = sem("wext_ready")
        stats_done = sem("stats_done")
        mv_done = sem("mv_done")
        veps_ready = sem("veps_ready")
        rstd_ready = sem("rstd_ready")
        nmr_ready = sem("nmr_ready")
        h_ready = sem("h_ready")
        h_transposed = sem("h_transposed")
        hT_ready = sem("hT_ready")
        wh_done = sem("wh_done")
        wh_stored = sem("wh_stored")
        row_done = sem("row_done")
        row_stored = sem("row_stored")
        hsum_step = sem("hsum_step")
        mean_done = sem("mean_done")
        mean_ready = sem("mean_ready")
        s12_ready = sem("s12_ready")
        mm_step = sem("mm_step")
        mm_transposed = sem("mm_transposed")
        mm_spread = sem("mm_spread")
        mmB_ready = sem("mmB_ready")
        exps_in = sem("exps_in")
        exps_ready = sem("exps_ready")
        ok_step = sem("ok_step")
        flag_ready = sem("flag_ready")
        prodA_ready = sem("prodA_ready")
        prodB_ready = sem("prodB_ready")
        highA_ready = sem("highA_ready")
        highB_ready = sem("highB_ready")
        ya_ready = sem("ya_ready")
        yb_ready = sem("yb_ready")
        signs_ready = sem("signs_ready")
        v_ready = sem("v_ready")
        v_transposed = sem("v_transposed")
        bt_ready = sem("bt_ready")
        at_ready = sem("at_ready")
        half_summed = sem("half_summed")
        partB_ready = sem("partB_ready")
        end_step = sem("end_step")
        sums_read = sem("sums_read")
        neg_ready = sem("neg_ready")
        eneg_ready = sem("eneg_ready")
        res_ready = sem("res_ready")
        out_stored = sem("out_stored")
        res_free = sem("res_free")
        g_row_done = sem("g_row_done")
        g_row_stored = sem("g_row_stored")
        g_loaded = sem("g_loaded")
        g_step = sem("g_step")
        g_p_ready = sem("g_p_ready")
        g_transposed = sem("g_transposed")
        g_pt_ready = sem("g_pt_ready")
        g_summed = sem("g_summed")
        g_end_step = sem("g_end_step")
        g_neg_ready = sem("g_neg_ready")
        g_eneg_ready = sem("g_eneg_ready")
        g_res_ready = sem("g_res_ready")
        g_stored = sem("g_stored")

        def slots(w):
            return slice(w * B, (w + 1) * B)

        def per_slot(a, n):
            return a.unsqueeze(2).to_broadcast([P, B, n])

        def fp8_slot(words, b):
            return words.bitcast(fp8).rearrange("p (i b) -> p i b", b=B)[:, :, b]

        block = ctx.enter_context(nc.Block())

        @block.sync
        def _(sp):
            for i in range(NX):
                n = G // NX
                sp.dma_start(x_sb[:, i * S // NX:(i + 1) * S // NX, :].rearrange("p (w b) d -> p w (b d)", b=B),
                             x_v[:, i * n:(i + 1) * n, :]).then_inc(x_loaded[i], 16)
            for t in range(TILES):
                sp.dma_start(adj_sb[:, t, :], adj_v[0, t]).then_inc(adj_loaded[t], 16)
            sp.wait_ge(flag_ready, 1)
            usual = sp.value_load(flag[0:1, 0:1], min_val=0, max_val=1)
            with sp.If(usual > 0):
                with sp.Fori(1, G) as w:
                    for b in range(B):
                        sp.wait_ge(v_ready, w * GH - GH + H * (b + 1))
                        sp.dma_start(adj_sb[:, b, :], adj_v[w, b]).then_inc(adj_loaded[b], 16)
            with sp.Else():
                for t in range(TILES):
                    sp.wait_ge(adj_loaded[t], 16)

                def general_group(w, first):
                    for b in range(B):
                        if not first or b:
                            sp.wait_ge(g_step, w * (B * 5) + b * 5)
                        sp.dma_start(g_adj, adj_v[w, b]).then_inc(g_loaded, 16)
                    sp.wait_ge(g_res_ready, w * B + B)
                    sp.dma_start(out_v[w], res.rearrange("p s d -> p (s d)")).then_inc(g_stored, 16)

                general_group(0, True)
                with sp.Fori(1, G) as w:
                    general_group(w, False)
                sp.wait_ge(g_stored, 16 * G)

        @block.gpsimd
        def _(pool):
            pool.memset(ones[:, :], 1.0).then_inc(consts_set, 1)
            pool.memset(half[:, :], 0.5).then_inc(consts_set, 1)
            pool.memset(minushalf[:, :], -0.5).then_inc(consts_set, 1)
            pool.memset(Wh[:, :, D:C], DEN_SCALE).then_inc(consts_set, 1)
            pool.memset(meanS[:, D:C], DEN_SCALE).then_inc(consts_set, 1)
            pool.memset(ident[:, :], 0.0).then_inc(consts_set, 1)
            pool.wait_ge(consts_set, 6)
            pool.affine_select(out=ident[:, :], in_=ident[:, :], compare_op=ALU.not_equal, fill=1.0,
                               base=0, pattern=[[-1, P]], channel_multiplier=1).then_inc(ident_ready, 1)
            pool.wait_ge(ssq_read, 1)
            pool.tensor_tensor(norm[:, :], norm[:, :], half[:, :], ALU.pow).then_inc(norm_ready, 1)
            n = S // NX
            for i in range(NX):
                q = slice(i * n, (i + 1) * n)
                pool.wait_ge(veps_ready, i + 1)
                pool.tensor_tensor(rstd[:, q], veps[:, q], minushalf[:, q], ALU.pow).then_inc(rstd_ready, 1)
            pool.wait_ge(flag_ready, 1)
            usual = pool.value_load(flag[0:1, 0:1], min_val=0, max_val=1)
            with pool.If(usual > 0):
                pool.wait_ge(exps_ready, 3)
                pool.wait_ge(wh_stored, G)
                pool.wait_ge(h_transposed, G)
                for w in range(G):
                    if w >= 2:
                        pool.wait_ge(yb_ready, w - 1)
                    pool.tensor_tensor(prodB[:, w % 2], Wh[:, slots(w), :], per_slot(F2[:, slots(w)], C),
                                       ALU.mult).then_inc(prodB_ready, 1)
                    pool.wait_ge(highB_ready, w + 1)
                    pool.wait_ge(prodB_ready, w + 1)
                    pool.tensor_tensor(YB[:, slots(w), C:2 * C], prodB[:, w % 2], YB[:, slots(w), 0:C],
                                       ALU.subtract).then_inc(yb_ready, 1)
                pool.sem_inc(res_free, 1)
                with pool.Fori(0, G) as w:
                    pool.wait_ge(res_ready, w + 1)
                    pool.dma_start(out_v[w], res.rearrange("p s d -> p (s d)")).then_inc(out_stored, 16)
                    pool.wait_ge(out_stored, w * 16 + 16)
                    pool.sem_inc(res_free, 1)

        @block.vector
        def _(dve):
            dve.wait_ge(w_loaded, 16)
            dve.tensor_tensor(wtmp[:, :], W_sb[:, :], W_sb[:, :], ALU.mult).then_inc(wsq_ready, 1)
            dve.wait_ge(a_loaded, 32)
            dve.wait_ge(consts_set, 6)
            for a in range(2):
                if a:
                    dve.wait_ge(wa_step, 2)
                dve.tensor_tensor(hsumrep[:, :], W_sb[:, :], a_sb[:, a, :], ALU.mult).then_inc(wa_step, 1)
                dve.wait_ge(wa_step, 2 * a + 1)
                dve.tensor_reduce(Wext[:, D + a:D + a + 1], hsumrep[:, :], AX.X, ALU.add).then_inc(wa_step, 1)
            dve.wait_ge(wa_step, 4)
            for a in range(2):
                dve.tensor_scalar(warep[:, a, :], ones[:, :], Wext[:, D + a:D + a + 1], None,
                                  ALU.mult).then_inc(wext_ready, 1)
            dve.wait_ge(ssq_done, 1)
            dve.tensor_scalar(norm[:, :], PMISC[:, 0:D], SSQ_MIN, None, ALU.max).then_inc(ssq_read, 1)
            dve.tensor_reduce(ssq_lim[:, 0:1], PMISC[:, 0:D], AX.X, ALU.min).then_inc(ok_step, 1)
            dve.tensor_reduce(ssq_lim[:, 1:2], PMISC[:, 0:D], AX.X, ALU.max).then_inc(ok_step, 1)

            def row_stats(i):
                n = S // NX
                dve.wait_ge(x_loaded[i], 16)
                for s in range(i * n, (i + 1) * n):
                    dve.bn_stats(stats[:, s, :], x_sb[:, s, :]).then_inc(stats_done, 1)
                for s in range(i * n, (i + 1) * n):
                    dve.wait_ge(stats_done, s + 1)
                    dve.bn_aggr(mv[:, s, :], stats[:, s, :]).then_inc(mv_done, 1)
                dve.wait_ge(mv_done, (i + 1) * n)
                dve.tensor_scalar(veps[:, i * n:(i + 1) * n], mv[:, i * n:(i + 1) * n, 1], EPS, None,
                                  ALU.add).then_inc(veps_ready, 1)

            def row_shift(i):
                q = slice(i * (S // NX), (i + 1) * (S // NX))
                dve.wait_ge(rstd_ready, i + 1)
                dve.scalar_tensor_tensor(nmr[:, q], mv[:, q, 0], -1.0, rstd[:, q], ALU.mult,
                                         ALU.mult).then_inc(nmr_ready, 1)

            row_stats(0)
            dve.wait_ge(norm_ready, 1)
            dve.tensor_scalar(unscale[:, :].bitcast(i32), norm[:, :].bitcast(i32), 0x7F800000, None,
                              ALU.bitwise_and).then_inc(scale_step, 1)
            dve.wait_ge(scale_step, 1)
            dve.reciprocal(wtmp[:, :], unscale[:, :]).then_inc(scale_step, 1)
            dve.wait_ge(scale_step, 2)
            dve.scalar_tensor_tensor(Wext[:, 0:D], wtmp[:, :], WH_SCALE, W_sb[:, :], ALU.mult,
                                     ALU.mult).then_inc(wext_ready, 1)
            dve.tensor_scalar(unscale[:, :], unscale[:, :], DEN_SCALE / WH_SCALE, None,
                              ALU.mult).then_inc(scale_step, 1)
            row_shift(0)
            for i in range(1, NX):
                row_stats(i)
                row_shift(i)

            for w in range(G):
                dve.wait_ge(wh_done, w + 1)
                dve.tensor_copy(Wh[:, slots(w), 0:D], PA[w % 2][:, 0:B * D].rearrange(
                    "p (s d) -> p s d", s=B)).then_inc(wh_stored, 1)
                dve.wait_ge(row_done, w + 1)
                dve.tensor_copy(s1row[:, w * GC:(w + 1) * GC], PB[w % 2][:, :]).then_inc(row_stored, 1)
            dve.tensor_copy(s12[:, :, :], PS12[:, 0:2 * S].rearrange("p (s a) -> p s a", a=2)).then_inc(s12_ready, 1)
            dve.wait_ge(s12_ready, 1)
            dve.tensor_reduce(mm[:, 0:1], s12[:, :, 1], AX.X, ALU.max).then_inc(mm_step, 1)
            dve.tensor_reduce(mm[:, 1:2], s12[:, :, 1], AX.X, ALU.min, negate=True).then_inc(mm_step, 1)
            dve.wait_ge(mm_transposed, 1)
            dve.tensor_reduce(mmT[:, :], PMISC[0:2, 0:P], AX.X, ALU.max).then_inc(mm_step, 1)
            dve.wait_ge(mm_step, 3)
            dve.tensor_scalar(mmD[:, :], ident[0:2, 0:2], mmT[:, :], None, ALU.mult).then_inc(mm_step, 1)
            dve.wait_ge(mm_spread, 1)
            dve.tensor_copy(mmB[:, :], PMISC[:, 0:2]).then_inc(mmB_ready, 1)
            dve.wait_ge(mmB_ready, 1)
            dve.tensor_scalar(sF[:, :], s12[:, :, 1], mmB[:, 0:1], None, ALU.subtract).then_inc(exps_in, 1)
            dve.tensor_scalar(u08[:, 0, :], s12[:, :, 0], mmB[:, 0:1], 1.0 - ALPHA, ALU.add,
                              ALU.mult).then_inc(exps_in, 1)
            dve.wait_ge(exps_in, 2)
            dve.tensor_scalar(u08[:, 1, :], u08[:, 0, :], -1.0, 0.0, ALU.mult, ALU.min).then_inc(exps_in, 1)
            dve.wait_ge(exps_in, 3)
            dve.tensor_scalar(u08[:, 0, :], u08[:, 0, :], 0.0, None, ALU.min).then_inc(exps_in, 1)
            dve.tensor_tensor(ok[:, 0:1], mmB[:, 0:1], mmB[:, 1:2], ALU.add).then_inc(ok_step, 1)
            dve.wait_ge(ok_step, 3)
            dve.tensor_scalar(ok[:, 1:2], ok[:, 0:1], SPREAD, None, ALU.is_le).then_inc(ok_step, 1)
            dve.wait_ge(ok_step, 4)
            dve.scalar_tensor_tensor(ok[:, 2:3], ssq_lim[:, 0:1], SSQ_MIN, ok[:, 1:2], ALU.is_ge,
                                     ALU.mult).then_inc(ok_step, 1)
            dve.wait_ge(ok_step, 5)
            dve.scalar_tensor_tensor(flag[:, :], ssq_lim[:, 1:2], SSQ_MAX, ok[:, 2:3], ALU.is_le,
                                     ALU.mult).then_inc(flag_ready, 1)
            dve.wait_ge(hT_ready, G)
            dve.tensor_reduce(hsum1[:, :], hsum[:, :], AX.X, ALU.add).then_inc(hsum_step, 1)
            dve.wait_ge(hsum_step, 1)
            dve.tensor_scalar(hsumrep[:, :], ones[:, :], hsum1[:, :], 1.0 / N, ALU.mult,
                              ALU.mult).then_inc(hsum_step, 1)
            dve.wait_ge(mean_done, 1)
            dve.tensor_copy(meanS[:, 0:D], PMISC[:, 0:D]).then_inc(mean_ready, 1)

            dve.wait_ge(flag_ready, 1)
            usual = dve.value_load(flag[0:1, 0:1], min_val=0, max_val=1)
            with dve.If(usual > 0):
                def code_edges(w, b, hf):
                    dve.wait_ge(adj_loaded[b], w * 16 + 16)
                    dve.tensor_scalar(V[:, hf, :], adj_sb[:, b, hf * HC:(hf + 1) * HC], 0.0, float(EDGE),
                                      ALU.is_gt, ALU.mult).then_inc(v_ready, 1)

                for hf in range(H):
                    code_edges(0, 0, hf)
                dve.wait_ge(exps_ready, 2)
                dve.wait_ge(h_transposed, G)
                for w in range(G):
                    if w >= 2:
                        dve.wait_ge(ya_ready, w - 1)
                    dve.tensor_tensor(prodA[:, w % 2], Wh[:, slots(w), :], per_slot(F1[:, slots(w)], C),
                                      ALU.mult).then_inc(prodA_ready, 1)
                    dve.wait_ge(highA_ready, w + 1)
                    dve.wait_ge(prodA_ready, w + 1)
                    dve.tensor_tensor(YA[:, slots(w), C:2 * C], prodA[:, w % 2], YA[:, slots(w), 0:C],
                                      ALU.subtract).then_inc(ya_ready, 1)

                END = 2 * B + 4

                def add_sums(w, b):
                    dve.wait_ge(partB_ready, w * B + b + 1)
                    dve.scalar_tensor_tensor(both[:, b, :], PA[b % 2][:, 0:2 * C], E[:, 0, bass.ds(w * B + b, 1)],
                                             partB[:, b, :], ALU.mult, ALU.add).then_inc(sums_read, 1)

                def divide(w):
                    e = w * END
                    dve.wait_ge(sums_read, w * B + B + 1)
                    dve.tensor_tensor(num, both[:, :, 0:C], both[:, :, C:2 * C], ALU.add).then_inc(end_step, 1)
                    dve.wait_ge(end_step, e + 1)
                    dve.tensor_scalar(nonei[:, :], num[:, :, D], 0.0, None, ALU.is_equal).then_inc(end_step, 1)
                    dve.wait_ge(end_step, e + 2)
                    for b in range(B):
                        dve.scalar_tensor_tensor(num[:, b, :], meanS[:, :], nonei[:, b:b + 1], num[:, b, :],
                                                 ALU.mult, ALU.add).then_inc(end_step, 1)
                    dve.wait_ge(end_step, e + 2 + B)
                    dve.reciprocal(rec[:, :], num[:, :, D]).then_inc(end_step, 1)
                    dve.wait_ge(end_step, e + 3 + B)
                    for b in range(B):
                        dve.scalar_tensor_tensor(hp[:, b, :], num[:, b, 0:D], rec[:, b:b + 1], unscale[:, :],
                                                 ALU.mult, ALU.mult).then_inc(end_step, 1)

                def split_sign(w):
                    dve.wait_ge(end_step, w * END + 3 + 2 * B)
                    dve.tensor_scalar(eneg, hp, 0.0, None, ALU.min).then_inc(neg_ready, 1)
                    dve.wait_ge(neg_ready, w + 1)
                    dve.scalar_tensor_tensor(hp, hp, 0.0, x_sb[:, bass.ds(w * B, B), :], ALU.max,
                                             ALU.add).then_inc(end_step, 1)

                def finish(w):
                    dve.wait_ge(end_step, w * END + 4 + 2 * B)
                    dve.wait_ge(eneg_ready, w + 1)
                    dve.wait_ge(res_free, w + 1)
                    dve.scalar_tensor_tensor(res, eneg, -1.0, hp, ALU.add, ALU.add).then_inc(res_ready, 1)

                def group(w, first, last):
                    for r in range(GH):
                        b, hf = r // H, r % H
                        k = w * GH + r
                        words = TP[hf][:, :].bitcast(i32).rearrange("p (v i) -> p v i", v=HG)
                        dve.wait_ge(v_transposed, k + 1)
                        dve.wait_ge(signs_ready, w * S + (hf + 1) * HS)
                        signs = T32[:, w % 2, hf * HG:(hf + 1) * HG, b * P:(b + 1) * P]
                        dve.tensor_tensor(BT[:, hf], words, signs, ALU.bitwise_and).then_inc(bt_ready, 1)
                        if not (last and r + H >= GH):
                            code_edges(w + (r + H) // GH, (b + 1) % B, hf)
                        dve.wait_ge(bt_ready, k + 1)
                        dve.tensor_tensor(AT[:, hf], words, BT[:, hf], ALU.bitwise_xor).then_inc(at_ready, 1)
                        if r == 1 and not first:
                            add_sums(w - 1, B - 1)
                        if r == 2 and not first:
                            divide(w - 1)
                        if r == 4 and not first:
                            split_sign(w - 1)
                        if r % H == 1 and r > 1:
                            add_sums(w, r // H - 1)
                        if r == GH - 1 and not first:
                            finish(w - 1)

                dve.wait_ge(mean_ready, 1)
                dve.sem_inc(sums_read, 1)
                group(0, True, False)
                with dve.Fori(1, G - 1) as w:
                    group(w, False, False)
                group(G - 1, False, True)
                add_sums(G - 1, B - 1)
                divide(G - 1)
                split_sign(G - 1)
                finish(G - 1)
            with dve.Else():
                dve.wait_ge(adj_loaded[3], 16)
                for w in range(G):
                    dve.wait_ge(g_row_done, w + 1)
                    dve.tensor_copy(g_s2row[:, w * GC:(w + 1) * GC].rearrange("m (p b) -> m b p", b=B),
                                    PB[w % 2][:, :].rearrange("m (b p) -> m b p", b=B)).then_inc(g_row_stored, 1)
                dve.wait_ge(g_row_stored, G)
                dve.wait_ge(adj_loaded[1], 16)
                dve.wait_ge(adj_loaded[2], 16)

                def general_group(w, first):
                    for b in range(B):
                        k = w * B + b
                        s = bass.ds(w * B + b, 1)
                        g = k * 5
                        if not first or b:
                            dve.wait_ge(g_p_ready, k)
                        dve.tensor_scalar(g_e, g_s2row, s12[:, s, 0], None, ALU.add).then_inc(g_step, 1)
                        dve.wait_ge(g_step, g + 1)
                        dve.scalar_tensor_tensor(g_e, g_e, ALPHA, g_e, ALU.mult, ALU.max).then_inc(g_step, 1)
                        dve.wait_ge(g_loaded, k * 16 + 16)
                        if not first or b:
                            dve.wait_ge(g_transposed, k * G)
                        dve.tensor_scalar(g_m, g_adj, 0.0, -1.0, ALU.is_gt, ALU.add).then_inc(g_step, 1)
                        dve.wait_ge(g_step, g + 3)
                        dve.scalar_tensor_tensor(g_e, g_m, -NEG_INF, g_e, ALU.mult, ALU.add).then_inc(g_step, 1)
                        dve.wait_ge(g_step, g + 4)
                        dve.tensor_reduce(g_nmax[:, :], g_e, AX.X, ALU.max, negate=True).then_inc(g_step, 1)
                        for i in range(G):
                            dve.wait_ge(g_transposed, k * G + i + 1)
                            if i >= 2:
                                dve.wait_ge(g_summed, k * G + i - 1)
                            dve.tensor_copy(g_PT[:, i % 2, :], TP[i % 2][:, :]).then_inc(g_pt_ready, 1)
                        h = k * 5
                        dve.wait_ge(g_summed, k * G + G)
                        dve.tensor_scalar(g_rec[:, :], g_den[:, :], DEN_SCALE, None, ALU.mult).then_inc(g_end_step, 1)
                        dve.wait_ge(g_end_step, h + 1)
                        dve.reciprocal(g_rec[:, :], g_rec[:, :]).then_inc(g_end_step, 1)
                        dve.wait_ge(g_end_step, h + 2)
                        dve.scalar_tensor_tensor(g_hp[:, b, :], PA[0][:, 0:D], g_rec[:, :], unscale[:, :], ALU.mult,
                                                 ALU.mult).then_inc(g_end_step, 1)
                        dve.wait_ge(g_end_step, h + 3)
                        dve.tensor_scalar(eneg[:, b, :], g_hp[:, b, :], 0.0, None, ALU.min).then_inc(g_neg_ready, 1)
                        dve.wait_ge(g_neg_ready, k + 1)
                        dve.tensor_scalar(g_hp[:, b, :], g_hp[:, b, :], 0.0, -1.0, ALU.max,
                                          ALU.add).then_inc(g_end_step, 1)
                        dve.wait_ge(g_end_step, h + 4)
                        dve.tensor_tensor(g_hp[:, b, :], g_hp[:, b, :], x_sb[:, s, :].rearrange("p s d -> p (s d)"),
                                          ALU.add).then_inc(g_end_step, 1)
                        dve.wait_ge(g_end_step, h + 5)
                        dve.wait_ge(g_eneg_ready, k + 1)
                        if b == 0 and not first:
                            dve.wait_ge(g_stored, w * 16)
                        dve.tensor_tensor(res[:, b, :], g_hp[:, b, :], eneg[:, b, :],
                                          ALU.add).then_inc(g_res_ready, 1)

                general_group(0, True)
                with dve.Fori(1, G) as w:
                    general_group(w, False)

        @block.scalar
        def _(act):
            act.dma_start(W_sb[:, :], W[:, :]).then_inc(w_loaded, 16)
            act.dma_start(a_sb[:, 0, :], a1.partition_broadcast(P)).then_inc(a_loaded, 16)
            act.dma_start(a_sb[:, 1, :], a2.partition_broadcast(P)).then_inc(a_loaded, 16)

            def store_hT(w):
                act.wait_ge(h_transposed, w + 1)
                act.activation(hT[:, slots(w), :], TP[w % 2][:, :].rearrange("p (s q) -> p s q", s=B), ACT.Copy,
                               accum_out=hsum[:, w:w + 1]).then_inc(hT_ready, 1)

            for w in range(G):
                act.wait_ge(nmr_ready, w * NX // G + 1)
                if w >= 2:
                    act.wait_ge(h_transposed, w - 1)
                for b in range(B):
                    s = w * B + b
                    act.activation(h_sb[:, w % 2, b, :], x_sb[:, s, :], ACT.Relu, bias=nmr[:, s:s + 1],
                                   scale=rstd[:, s:s + 1]).then_inc(h_ready, 1)
                if w:
                    store_hT(w - 1)
            store_hT(G - 1)
            act.wait_ge(exps_in, 2)
            act.activation(F1[:, :], sF[:, :], ACT.Exp).then_inc(exps_ready, 1)
            act.activation(F2[:, :], sF[:, :], ACT.Exp, scale=ALPHA).then_inc(exps_ready, 1)
            act.wait_ge(exps_in, 4)
            act.activation(E[:, :, :], u08[:, :, :], ACT.Exp).then_inc(exps_ready, 1)

            act.wait_ge(flag_ready, 1)
            usual = act.value_load(flag[0:1, 0:1], min_val=0, max_val=1)
            with act.If(usual > 0):
                def signs(w, first, last):
                    for s in range(first, last):
                        act.activation(T8[:, w % 2, s // B, :, s % B], s1row[:, bass.ds(w * GC, GC)], ACT.Sign,
                                       bias=s12[:, s, 1:2]).then_inc(signs_ready, 1)

                act.wait_ge(wh_done, G)
                act.wait_ge(row_stored, G)
                act.wait_ge(mean_done, 1)
                for w in range(G):
                    act.wait_ge(prodA_ready, w + 1)
                    act.activation(YA[:, slots(w), 0:C], prodA[:, w % 2], ACT.Copy).then_inc(highA_ready, 1)
                    act.wait_ge(prodB_ready, w + 1)
                    act.activation(YB[:, slots(w), 0:C], prodB[:, w % 2], ACT.Copy).then_inc(highB_ready, 1)
                    signs(0, w * B, (w + 1) * B)

                def scale_sums(w, b):
                    act.wait_ge(half_summed, w * GH + H * (b + 1))
                    act.activation(partB[:, b, :], PB[b % 2][:, 0:2 * C], ACT.Copy,
                                   scale=E[:, 1, bass.ds(w * B + b, 1)]).then_inc(partB_ready, 1)

                def end_exp(w):
                    act.wait_ge(neg_ready, w + 1)
                    act.activation(eneg, eneg, ACT.Exp).then_inc(eneg_ready, 1)

                def group(w, first, last):
                    q = S // B
                    if not last:
                        if not first:
                            act.wait_ge(bt_ready, w * GH)
                        signs(w + 1, 0, q)
                    for b in range(B - 1):
                        if not last:
                            signs(w + 1, (b + 1) * q, (b + 2) * q)
                        act.wait_ge(sums_read, w * B + 1)
                        scale_sums(w, b)
                        if b == 1 and not first:
                            end_exp(w - 1)
                    scale_sums(w, B - 1)

                group(0, True, False)
                with act.Fori(1, G - 1) as w:
                    group(w, False, False)
                group(G - 1, False, True)
                end_exp(G - 1)
            with act.Else():
                with act.Fori(0, G) as w:
                    for b in range(B):
                        k = w * B + b
                        act.wait_ge(g_step, k * 5 + 5)
                        act.activation(g_m, g_e, ACT.Exp, bias=g_nmax[:, :],
                                       accum_out=g_den[:, :]).then_inc(g_p_ready, 1)
                        act.wait_ge(g_neg_ready, k + 1)
                        act.activation(eneg[:, b, :], eneg[:, b, :], ACT.Exp).then_inc(g_eneg_ready, 1)

        @block.tensor
        def _(pe):
            pe.wait_ge(consts_set, 6)
            pe.wait_ge(wsq_ready, 1)
            nc.tensor.matmul(PMISC[:, 0:D], ones[:, :], wtmp[:, :], start=True, stop=True).then_inc(ssq_done, 1)
            pe.wait_ge(ident_ready, 1)

            def turn_h(w):
                pe.wait_ge(h_ready, (w + 1) * B)
                if w >= 2:
                    pe.wait_ge(hT_ready, w - 1)
                for b in range(B):
                    t = nc.tensor.transpose(TP[w % 2][:, b * P:(b + 1) * P], h_sb[:, w % 2, b, :], ident[:, :])
                t.then_inc(h_transposed, 1)

            def project(w):
                pe.wait_ge(hT_ready, w + 1)
                pe.wait_ge(wext_ready, 3)
                if w >= 2:
                    pe.wait_ge(wh_stored, w - 1)
                    pe.wait_ge(row_stored, w - 1)
                for b in range(B):
                    s = w * B + b
                    nc.tensor.matmul(PA[w % 2][:, b * D:(b + 1) * D], hT[:, s, :], Wext[:, 0:D],
                                     start=True, stop=True)
                    t = nc.tensor.matmul(PS12[:, 2 * s:2 * s + 2], hT[:, s, :], Wext[:, D:D + 2],
                                         start=True, stop=True)
                t.then_inc(wh_done, 1)
                nc.tensor.matmul(PB[w % 2][:, :], warep[:, 0, :], hT[:, slots(w), :].rearrange("p s q -> p (s q)"),
                                 start=True, stop=True).then_inc(row_done, 1)

            turn_h(0)
            for w in range(G):
                if w + 1 < G:
                    turn_h(w + 1)
                project(w)
            pe.wait_ge(mm_step, 2)
            pe.wait_ge(ok_step, 2)
            nc.tensor.transpose(PMISC[0:2, 0:P], mm[:, :], ident[:, :]).then_inc(mm_transposed, 1)
            pe.wait_ge(mm_step, 4)
            nc.tensor.matmul(PMISC[:, 0:2], ones[0:2, :], mmD[:, :], start=True, stop=True).then_inc(mm_spread, 1)
            pe.wait_ge(hsum_step, 2)
            pe.wait_ge(mmB_ready, 1)
            nc.tensor.matmul(PMISC[:, 0:D], hsumrep[:, :], Wext[:, 0:D], start=True, stop=True).then_inc(mean_done, 1)

            pe.wait_ge(flag_ready, 1)
            usual = pe.value_load(flag[0:1, 0:1], min_val=0, max_val=1)
            with pe.If(usual > 0):
                def turn_words(k, hf):
                    pe.wait_ge(v_ready, k + 1)
                    for v in range(HG):
                        t = nc.tensor.transpose(TP[hf][:, v * P:(v + 1) * P],
                                                V[:, hf, v * GC:(v + 1) * GC].bitcast(f32), ident[:, :])
                    t.then_inc(v_transposed, 1)

                def wait_for_half(w, r):
                    pe.wait_ge(bt_ready, w * GH + r + 1)
                    pe.wait_ge(at_ready, w * GH + r + 1)
                    if r % H == 0:
                        pe.wait_ge(sums_read, w * B + r // H)

                def group(w, last):
                    for r in range(GH):
                        b, hf = r // H, r % H
                        for v in range(HG):
                            g = hf * HG + v
                            if b == 0:
                                pe.wait_ge(ya_ready, g + 1)
                                pe.wait_ge(yb_ready, g + 1)
                            for j in range(B):
                                first, end = (g == 0 and j == 0), (g == G - 1 and j == B - 1)
                                nc.tensor.matmul(PA[b % 2][:, 0:2 * C], fp8_slot(AT[:, hf, v, :], j),
                                                 YA[:, g * B + j, :], start=first, stop=end)
                                t = nc.tensor.matmul(PB[b % 2][:, 0:2 * C], fp8_slot(BT[:, hf, v, :], j),
                                                     YB[:, g * B + j, :], start=first, stop=end)
                        t.then_inc(half_summed, 1)
                        if not (last and r + 1 == GH):
                            wait_for_half(w, r + 1)
                        if not (last and r + H >= GH):
                            turn_words(w * GH + r + H, hf)

                pe.wait_ge(hT_ready, G)
                pe.wait_ge(wh_stored, G)
                pe.wait_ge(row_stored, G)
                turn_words(0, 0)
                turn_words(1, 1)
                pe.wait_ge(bt_ready, 1)
                pe.wait_ge(at_ready, 1)
                with pe.Fori(0, G - 1) as w:
                    group(w, False)
                group(G - 1, True)
            with pe.Else():
                for w in range(G):
                    pe.wait_ge(row_stored, G)
                    if w >= 2:
                        pe.wait_ge(g_row_stored, w - 1)
                    nc.tensor.matmul(PB[w % 2][:, :], warep[:, 1, :], hT[:, slots(w), :].rearrange(
                        "p s q -> p (s q)"), start=True, stop=True).then_inc(g_row_done, 1)

                def general_group(w, first):
                    for b in range(B):
                        k = w * B + b
                        pe.wait_ge(g_p_ready, k + 1)
                        if not first or b:
                            pe.wait_ge(g_pt_ready, k * G)
                            pe.wait_ge(g_end_step, k * 5)

                        def turn(i):
                            if i >= 2:
                                pe.wait_ge(g_pt_ready, k * G + i - 1)
                            cols = g_m[:, i * GC:(i + 1) * GC].rearrange("i (q c) -> i q c", c=B)
                            for j in range(B):
                                t = nc.tensor.transpose(TP[i % 2][:, j * P:(j + 1) * P], cols[:, :, j], ident[:, :])
                            t.then_inc(g_transposed, 1)

                        turn(0)
                        for i in range(G):
                            if i + 1 < G:
                                turn(i + 1)
                            pe.wait_ge(g_pt_ready, k * G + i + 1)
                            for j in range(B):
                                t = nc.tensor.matmul(PA[0][:, 0:D], g_PT[:, i % 2, j * P:(j + 1) * P],
                                                     Wh[:, i * B + j, 0:D], start=(i == 0 and j == 0),
                                                     stop=(i == G - 1 and j == B - 1))
                            t.then_inc(g_summed, 1)

                pe.wait_ge(wh_stored, G)
                general_group(0, True)
                with pe.Fori(1, G) as w:
                    general_group(w, False)


def kernel(x, adj, L0_gnn_W, L0_gnn_a1, L0_gnn_a2):
    import numpy as np
    import concourse.bacc as bacc
    from concourse import mybir
    from concourse.bass_utils import run_bass_kernel_spmd

    nc = bacc.Bacc("TRN2", target_bir_lowering=False, num_devices=1)
    arrays, args = {}, []
    for name, a in (("x", x), ("adj", adj), ("W", L0_gnn_W), ("a1", L0_gnn_a1), ("a2", L0_gnn_a2)):
        a = np.ascontiguousarray(a)
        arrays[f"in_{name}"] = a
        args.append(nc.dram_tensor(f"in_{name}", a.shape, mybir.dt.from_np(a.dtype), kind="ExternalInput").ap())
    out = nc.dram_tensor("out", x.shape, mybir.dt.float32, kind="ExternalOutput").ap()
    build(nc, *args, out)
    r = run_bass_kernel_spmd(nc, [arrays], core_ids=[0])
    return r.results[0]["out"]
```

```python
import concourse.bass as bass
from concourse import mybir
from contextlib import ExitStack


def build(nc, x, adj, adjT, W, a1, a2, out):
    f32, i32 = mybir.dt.float32, mybir.dt.int32
    f16, u8, i8, fp8 = mybir.dt.float16, mybir.dt.uint8, mybir.dt.int8, mybir.dt.float8e4
    ALU = mybir.AluOpType
    ACT = mybir.ActivationFunctionType
    AX = mybir.AxisListType

    N, D = x.shape
    P = 128
    B = 4
    G = N // (P * B)
    S = G * B
    GC = P * B
    H = 2
    HC = N // H
    HG = G // H
    HS = S // H
    GH = B * H
    C = D + 1
    TILES = B
    R = 4
    ALPHA = 0.2
    NEG_INF = -9000000000000000.0
    EPS = 1e-5
    SPREAD = 8.0
    EDGE = 8
    DEN_SCALE = 2.0 ** 14
    EXP_ONE = 2.0 ** 23
    SCALE_EXP = 127 + 11 - (64 - 127)
    UNSCALE_EXP = 127 + 14 + (64 - 127) - 11
    SSQ_MIN, SSQ_MAX = 1e-30, 1e30
    DVE_YB = (3, 6)
    POOL_YB = tuple(g for g in range(G) if g not in DVE_YB)

    x_v = x.rearrange("(w p b) d -> p w (b d)", p=P, b=B)
    out_v = out.rearrange("(w p b) d -> w p (b d)", p=P, b=B)
    adj_v = adj.rearrange("(w p b) j -> w b p j", p=P, b=B)

    ctx = ExitStack()
    with ctx:
        def sb(name, shape, dt):
            return ctx.enter_context(nc.sbuf_tensor(name, shape, dt))

        def sem(name):
            return ctx.enter_context(nc.semaphore(name))

        x_sb = sb("x_sb", [P, S, D], f32)
        T_mem = sb("T_mem", [P, 2 * N], f32)
        hT = T_mem[:, 0:N].rearrange("p (s q) -> p s q", q=P)
        T8 = T_mem[:, :].bitcast(i8).rearrange("p (r s i) -> p r s i", r=2, s=S)
        T32 = T_mem[:, :].bitcast(i32).rearrange("p (r s q) -> p r s q", r=2, s=S)
        s1row = sb("s1row", [P, N], f32)
        WhM = sb("WhM", [P, S * C], f32)
        Wh = WhM[:, :].rearrange("p (s c) -> p s c", c=C)
        partB = WhM[:, 0:B * 2 * C].rearrange("p (s c) -> p s c", s=B)
        both = WhM[:, B * 2 * C:2 * B * 2 * C].rearrange("p (s c) -> p s c", s=B)
        num = WhM[:, 4 * B * C:5 * B * C].rearrange("p (s c) -> p s c", s=B)
        hp = WhM[:, 5 * B * C:5 * B * C + B * D].rearrange("p (s d) -> p s d", s=B)
        YA = sb("YA", [P, S, 2 * C], f16)
        YB = sb("YB", [P, S, 2 * C], f16)
        adj_sb = sb("adj_sb", [P, TILES, N], i32)
        V = sb("V", [P, R, HC], u8)
        BT = sb("BT", [P, R, HC], u8)
        early = BT[:, R - 2:R, :].rearrange("p r c -> p (r c)").bitcast(f32)
        W_sb = early[:, 0:D]
        wsq = early[:, D:2 * D]
        expo = early[:, 2 * D:3 * D].bitcast(i32)
        scale = early[:, 3 * D:4 * D].bitcast(i32)
        a_sb = early[:, 4 * D:6 * D].rearrange("p (a d) -> p a d", a=2)
        scratch = sb("scratch", [P, 4 * B * C], f32)
        h_sb = scratch[:, 0:2 * GC].rearrange("p (r s d) -> p r s d", r=2, s=B)
        prodA = scratch[:, 0:2 * B * C].rearrange("p (r s c) -> p r s c", r=2, s=B)
        prodB = scratch[:, 2 * B * C:4 * B * C].rearrange("p (r s c) -> p r s c", r=2, s=B)
        eneg = scratch[:, 0:GC].rearrange("p (s d) -> p s d", s=B)
        res = scratch[:, GC:2 * GC].rearrange("p (s d) -> p s d", s=B)
        ident = sb("ident", [P, P], f32)
        ones = sb("ones", [P, P], f32)
        Wext = sb("Wext", [P, D + 2], f32)
        warep = sb("warep", [P, 2, P], f32)
        unscale = sb("unscale", [P, D], f32)
        minushalf = sb("minushalf", [P, S], f32)
        stats = sb("stats", [P, S, 6], f32)
        mv = sb("mv", [P, S, 2], f32)
        veps = sb("veps", [P, S], f32)
        rstd = sb("rstd", [P, S], f32)
        hsum = sb("hsum", [P, G], f32)
        hsum1 = sb("hsum1", [P, 1], f32)
        hsumrep = sb("hsumrep", [P, P], f32)
        meanS = sb("meanS", [P, C], f32)
        s12 = sb("s12", [P, S, 2], f32)
        mm = sb("mm", [P, 2], f32)
        mmT = sb("mmT", [2, 1], f32)
        mmD = sb("mmD", [2, 2], f32)
        mmB = sb("mmB", [P, 2], f32)
        sF = sb("sF", [P, S], f32)
        u08 = sb("u08", [P, 2, S], f32)
        F1 = sb("F1", [P, S], f32)
        F2 = sb("F2", [P, S], f32)
        E = sb("E", [P, 2, S], f32)
        ssq_lim = sb("ssq_lim", [P, 2], f32)
        ok = sb("ok", [P, 4], f32)
        flag = sb("flag", [P, 1], i32)
        nonei = sb("nonei", [P, B], f32)
        rec = sb("rec", [P, B], f32)
        g_adj = adj_sb[:, 0, :]
        g_e = adj_sb[:, 1, :].bitcast(f32)
        g_m = adj_sb[:, 2, :].bitcast(f32)
        g_s2row = adj_sb[:, 3, :].bitcast(f32)
        g_PT = YA[:, :, :].rearrange("p s c -> p (s c)")[:, 0:4 * GC].bitcast(f32).rearrange(
            "p (r c) -> p r c", r=2)
        g_hp = scratch[:, 2 * GC:3 * GC].rearrange("p (s d) -> p s d", s=B)
        g_nmax = sb("g_nmax", [P, 1], f32)
        g_den = sb("g_den", [P, 1], f32)
        g_rec = sb("g_rec", [P, 1], f32)

        def bank(name):
            return ctx.enter_context(nc.psum_tensor(name, [P, 512], f32))

        TP = [bank("TP0"), bank("TP1")]
        PA = [bank("PA0"), bank("PA1")]
        PB = [bank("PB0"), bank("PB1")]
        PMISC = bank("PMISC")
        PS12 = [bank("PS12"), PMISC]

        x_loaded = [sem(f"x_loaded{w}") for w in range(G)]
        w_loaded = sem("w_loaded")
        a_loaded = sem("a_loaded")
        adj_loaded = [sem(f"adj_loaded{i}") for i in range(TILES)]
        consts_set = sem("consts_set")
        ident_ready = sem("ident_ready")
        wsq_ready = sem("wsq_ready")
        ssq_done = sem("ssq_done")
        scale_step = sem("scale_step")
        wa_step = sem("wa_step")
        wext_ready = sem("wext_ready")
        stats_done = sem("stats_done")
        mv_done = sem("mv_done")
        veps_ready = sem("veps_ready")
        rstd_ready = sem("rstd_ready")
        h_ready = sem("h_ready")
        h_transposed = sem("h_transposed")
        hT_ready = sem("hT_ready")
        wh_done = sem("wh_done")
        wh_stored = sem("wh_stored")
        row_done = sem("row_done")
        row_stored = sem("row_stored")
        hsum_step = sem("hsum_step")
        mean_done = sem("mean_done")
        mean_ready = sem("mean_ready")
        s12_ready = sem("s12_ready")
        mm_step = sem("mm_step")
        mm_transposed = sem("mm_transposed")
        mm_spread = sem("mm_spread")
        mmB_ready = sem("mmB_ready")
        exps_in = sem("exps_in")
        exps_ready = sem("exps_ready")
        ok_step = sem("ok_step")
        flag_ready = sem("flag_ready")
        prodA_ready = sem("prodA_ready")
        prodB_ready = sem("prodB_ready")
        highA_ready = sem("highA_ready")
        highB_ready = sem("highB_ready")
        ya_ready = sem("ya_ready")
        yb_pool_ready = sem("yb_pool_ready")
        highB_dve_ready = sem("highB_dve_ready")
        yb_dve_ready = sem("yb_dve_ready")
        signs_ready = sem("signs_ready")
        v_ready = sem("v_ready")
        bt_ready = sem("bt_ready")
        at_ready = sem("at_ready")
        half_started = sem("half_started")
        half_summed = sem("half_summed")
        partB_ready = sem("partB_ready")
        end_step = sem("end_step")
        sums_read = sem("sums_read")
        neg_ready = sem("neg_ready")
        eneg_ready = sem("eneg_ready")
        res_ready = sem("res_ready")
        out_stored = sem("out_stored")
        res_free = sem("res_free")
        last_step = sem("last_step")
        last_neg_ready = sem("last_neg_ready")
        last_eneg_ready = sem("last_eneg_ready")
        last_res_ready = sem("last_res_ready")
        last_stored = sem("last_stored")
        g_row_done = sem("g_row_done")
        g_row_stored = sem("g_row_stored")
        g_loaded = sem("g_loaded")
        g_step = sem("g_step")
        g_p_ready = sem("g_p_ready")
        g_transposed = sem("g_transposed")
        g_pt_ready = sem("g_pt_ready")
        g_summed = sem("g_summed")
        g_end_step = sem("g_end_step")
        g_neg_ready = sem("g_neg_ready")
        g_eneg_ready = sem("g_eneg_ready")
        g_res_ready = sem("g_res_ready")
        g_stored = sem("g_stored")

        def slots(w):
            return slice(w * B, (w + 1) * B)

        def per_slot(a, n):
            return a.unsqueeze(2).to_broadcast([P, B, n])

        def half_words(m, r):
            return m[:, r % R, :].bitcast(i32).rearrange("p (s q) -> p s q", s=HS)

        def fp8_slot(m, r, j):
            return m[:, r % R, j * P:(j + 1) * P].bitcast(fp8)

        block = ctx.enter_context(nc.Block())

        @block.sync
        def _(sp):
            for w in range(G):
                sp.dma_start(x_sb[:, slots(w), :].rearrange("p b d -> p (b d)"), x_v[:, w, :]).then_inc(x_loaded[w], 16)
            for t in range(TILES):
                sp.dma_start(adj_sb[:, t, :], adjT[0, t]).then_inc(adj_loaded[t], 16)
            sp.wait_ge(flag_ready, 1)
            usual = sp.value_load(flag[0:1, 0:1], min_val=0, max_val=1)
            with sp.If(usual > 0):
                with sp.Fori(1, G) as w:
                    for b in range(B):
                        sp.wait_ge(v_ready, w * GH - GH + H * (b + 1))
                        sp.dma_start(adj_sb[:, b, :], adjT[w, b]).then_inc(adj_loaded[b], 16)
                for b in range(B):
                    sp.wait_ge(last_res_ready, b + 1)
                    sp.dma_start(out_v[G - 1][:, b * D:(b + 1) * D], res[:, b, :]).then_inc(last_stored, 16)
                sp.wait_ge(last_stored, 16 * B)
            with sp.Else():
                sp.wait_ge(v_ready, H)
                for t in range(TILES):
                    sp.wait_ge(adj_loaded[t], 16)

                def general_group(w, first):
                    for b in range(B):
                        if not first or b:
                            sp.wait_ge(g_step, w * (B * 5) + b * 5)
                        sp.dma_start(g_adj, adj_v[w, b]).then_inc(g_loaded, 16)
                    sp.wait_ge(g_res_ready, w * B + B)
                    sp.dma_start(out_v[w], res.rearrange("p s d -> p (s d)")).then_inc(g_stored, 16)

                general_group(0, True)
                with sp.Fori(1, G) as w:
                    general_group(w, False)
                sp.wait_ge(g_stored, 16 * G)

        @block.gpsimd
        def _(pool):
            pool.memset(ones[:, :], 1.0).then_inc(consts_set, 1)
            pool.memset(minushalf[:, :], -0.5).then_inc(consts_set, 1)
            pool.memset(Wh[:, :, D:C], DEN_SCALE).then_inc(consts_set, 1)
            pool.memset(meanS[:, D:C], DEN_SCALE).then_inc(consts_set, 1)
            pool.memset(ident[:, :], 0.0).then_inc(consts_set, 1)
            pool.wait_ge(consts_set, 5)
            pool.affine_select(out=ident[:, :], in_=ident[:, :], compare_op=ALU.not_equal, fill=1.0,
                               base=0, pattern=[[-1, P]], channel_multiplier=1).then_inc(ident_ready, 1)
            for w in range(G):
                pool.wait_ge(veps_ready, w + 1)
                pool.tensor_tensor(rstd[:, slots(w)], veps[:, slots(w)], minushalf[:, slots(w)],
                                   ALU.pow).then_inc(rstd_ready, 1)
            pool.wait_ge(flag_ready, 1)
            usual = pool.value_load(flag[0:1, 0:1], min_val=0, max_val=1)
            with pool.If(usual > 0):
                pool.wait_ge(exps_ready, 3)
                pool.wait_ge(wh_stored, G)
                pool.wait_ge(h_transposed, G)
                def product(n):
                    pool.tensor_tensor(prodB[:, n % 2], Wh[:, slots(POOL_YB[n]), :],
                                       per_slot(F2[:, slots(POOL_YB[n])], C), ALU.mult).then_inc(prodB_ready, 1)

                product(0)
                for n, w in enumerate(POOL_YB):
                    if n + 1 < len(POOL_YB):
                        if n:
                            pool.wait_ge(yb_pool_ready, n)
                        product(n + 1)
                    pool.wait_ge(highB_ready, n + 1)
                    pool.wait_ge(prodB_ready, n + 1)
                    pool.tensor_tensor(YB[:, slots(w), C:2 * C], prodB[:, n % 2], YB[:, slots(w), 0:C],
                                       ALU.subtract).then_inc(yb_pool_ready, 1)
                pool.sem_inc(res_free, 1)
                with pool.Fori(0, G - 1) as w:
                    pool.wait_ge(res_ready, w + 1)
                    pool.dma_start(out_v[w], res.rearrange("p s d -> p (s d)")).then_inc(out_stored, 16)
                    pool.wait_ge(out_stored, w * 16 + 16)
                    pool.sem_inc(res_free, 1)

        @block.vector
        def _(dve):
            def row_stats(w):
                dve.wait_ge(x_loaded[w], 16)
                for s in range(w * B, (w + 1) * B):
                    dve.bn_stats(stats[:, s, :], x_sb[:, s, :]).then_inc(stats_done, 1)
                for s in range(w * B, (w + 1) * B):
                    dve.wait_ge(stats_done, s + 1)
                    dve.bn_aggr(mv[:, s, :], stats[:, s, :]).then_inc(mv_done, 1)
                dve.wait_ge(mv_done, (w + 1) * B)
                dve.tensor_scalar(veps[:, slots(w)], mv[:, slots(w), 1], EPS, None, ALU.add).then_inc(veps_ready, 1)

            def normalise(w):
                dve.wait_ge(rstd_ready, w + 1)
                if w >= 2:
                    dve.wait_ge(h_transposed, w - 1)
                for b in range(B):
                    s = w * B + b
                    dve.tensor_scalar(h_sb[:, w % 2, b, :], x_sb[:, s, :], mv[:, s, 0:1], rstd[:, s:s + 1],
                                      ALU.subtract, ALU.mult).then_inc(h_ready, 1)

            dve.wait_ge(w_loaded, 16)
            dve.tensor_tensor(wsq[:, :], W_sb[:, :], W_sb[:, :], ALU.mult).then_inc(wsq_ready, 1)
            row_stats(0)
            dve.wait_ge(a_loaded, 32)
            dve.wait_ge(consts_set, 5)
            for a in range(2):
                if a:
                    dve.wait_ge(wa_step, 2)
                dve.tensor_tensor(hsumrep[:, :], W_sb[:, :], a_sb[:, a, :], ALU.mult).then_inc(wa_step, 1)
                dve.wait_ge(wa_step, 2 * a + 1)
                dve.tensor_reduce(Wext[:, D + a:D + a + 1], hsumrep[:, :], AX.X, ALU.add).then_inc(wa_step, 1)
            dve.wait_ge(wa_step, 4)
            for a in range(2):
                dve.tensor_scalar(warep[:, a, :], ones[:, :], Wext[:, D + a:D + a + 1], None,
                                  ALU.mult).then_inc(wext_ready, 1)
            dve.wait_ge(ssq_done, 1)
            dve.tensor_scalar(expo[:, :], PMISC[:, 0:D].bitcast(i32), 24, 23, ALU.logical_shift_right,
                              ALU.logical_shift_left).then_inc(scale_step, 1)
            dve.tensor_reduce(ssq_lim[:, 0:1], PMISC[:, 0:D], AX.X, ALU.min).then_inc(ok_step, 1)
            dve.tensor_reduce(ssq_lim[:, 1:2], PMISC[:, 0:D], AX.X, ALU.max).then_inc(ok_step, 1)
            dve.wait_ge(scale_step, 1)
            dve.tensor_scalar(scale[:, :], expo[:, :], -1.0, SCALE_EXP * EXP_ONE, ALU.mult,
                              ALU.add).then_inc(scale_step, 1)
            dve.tensor_scalar(unscale[:, :].bitcast(i32), expo[:, :], UNSCALE_EXP * EXP_ONE, None,
                              ALU.add).then_inc(scale_step, 1)
            dve.wait_ge(scale_step, 3)
            dve.tensor_tensor(Wext[:, 0:D], W_sb[:, :], scale[:, :].bitcast(f32), ALU.mult).then_inc(wext_ready, 1)

            def code_edges(w, r, early):
                dve.wait_ge(adj_loaded[r // H], w * 16 + 16)
                if not early:
                    dve.wait_ge(half_summed, w * GH + r - R + 1)
                dve.tensor_scalar(V[:, r % R, :], adj_sb[:, r // H, (r % H) * HC:(r % H + 1) * HC], 0.0, float(EDGE),
                                  ALU.is_gt, ALU.mult).then_inc(v_ready, 1)

            def mask_b(w, r):
                dve.wait_ge(v_ready, w * GH + r + 1)
                dve.wait_ge(signs_ready, w * S + (r % H + 1) * HS)
                signs = T32[:, (w + 1) % 2, (r % H) * HS:(r % H + 1) * HS, (r // H) * P // B:(r // H + 1) * P // B]
                dve.tensor_tensor(half_words(BT, r), half_words(V, r), signs, ALU.bitwise_and).then_inc(bt_ready, 1)

            def mask_a(w, r):
                dve.wait_ge(bt_ready, w * GH + r + 1)
                dve.tensor_tensor(half_words(V, r), half_words(V, r), half_words(BT, r),
                                  ALU.bitwise_xor).then_inc(at_ready, 1)

            row_stats(1)
            normalise(0)
            row_stats(2)
            normalise(1)
            for w in range(G):
                if w + 3 < G:
                    row_stats(w + 3)
                if w + 2 < G:
                    normalise(w + 2)
                dve.wait_ge(wh_done, w + 1)
                dve.tensor_copy(s12[:, slots(w), :], PS12[w % 2][:, 0:2 * B].rearrange(
                    "p (s a) -> p s a", a=2)).then_inc(s12_ready, 1)
                dve.tensor_copy(Wh[:, slots(w), 0:D], PA[w % 2][:, 0:B * D].rearrange(
                    "p (s d) -> p s d", s=B)).then_inc(wh_stored, 1)
                dve.wait_ge(row_done, w + 1)
                dve.tensor_copy(s1row[:, w * GC:(w + 1) * GC], PB[w % 2][:, :]).then_inc(row_stored, 1)
                if w >= G - H:
                    code_edges(0, w - (G - H), True)
            dve.wait_ge(s12_ready, G)
            dve.tensor_reduce(mm[:, 0:1], s12[:, :, 1], AX.X, ALU.max).then_inc(mm_step, 1)
            dve.tensor_reduce(mm[:, 1:2], s12[:, :, 1], AX.X, ALU.min, negate=True).then_inc(mm_step, 1)
            mask_b(0, 0)
            dve.wait_ge(mm_transposed, 1)
            dve.tensor_reduce(mmT[:, :], PMISC[0:2, 0:P], AX.X, ALU.max).then_inc(mm_step, 1)
            dve.wait_ge(mm_step, 3)
            dve.tensor_scalar(mmD[:, :], ident[0:2, 0:2], mmT[:, :], None, ALU.mult).then_inc(mm_step, 1)
            mask_a(0, 0)
            dve.wait_ge(mm_spread, 1)
            dve.tensor_copy(mmB[:, :], PMISC[:, 0:2]).then_inc(mmB_ready, 1)
            dve.wait_ge(mmB_ready, 1)
            dve.tensor_scalar(sF[:, :], s12[:, :, 1], mmB[:, 0:1], None, ALU.subtract).then_inc(exps_in, 1)
            dve.tensor_scalar(u08[:, 0, :], s12[:, :, 0], mmB[:, 0:1], 1.0 - ALPHA, ALU.add,
                              ALU.mult).then_inc(exps_in, 1)
            dve.wait_ge(exps_in, 2)
            dve.tensor_scalar(u08[:, 1, :], u08[:, 0, :], -1.0, 0.0, ALU.mult, ALU.min).then_inc(exps_in, 1)
            dve.wait_ge(exps_in, 3)
            dve.tensor_scalar(u08[:, 0, :], u08[:, 0, :], 0.0, None, ALU.min).then_inc(exps_in, 1)
            dve.tensor_tensor(ok[:, 0:1], mmB[:, 0:1], mmB[:, 1:2], ALU.add).then_inc(ok_step, 1)
            dve.wait_ge(ok_step, 3)
            dve.tensor_scalar(ok[:, 1:2], ok[:, 0:1], SPREAD, None, ALU.is_le).then_inc(ok_step, 1)
            dve.wait_ge(ok_step, 4)
            dve.scalar_tensor_tensor(ok[:, 2:3], ssq_lim[:, 0:1], SSQ_MIN, ok[:, 1:2], ALU.is_ge,
                                     ALU.mult).then_inc(ok_step, 1)
            dve.wait_ge(ok_step, 5)
            dve.scalar_tensor_tensor(flag[:, :], ssq_lim[:, 1:2], SSQ_MAX, ok[:, 2:3], ALU.is_le,
                                     ALU.mult).then_inc(flag_ready, 1)
            dve.wait_ge(hT_ready, G)
            dve.tensor_reduce(hsum1[:, :], hsum[:, :], AX.X, ALU.add).then_inc(hsum_step, 1)
            dve.wait_ge(hsum_step, 1)
            dve.tensor_scalar(hsumrep[:, :], ones[:, :], hsum1[:, :], 1.0 / N, ALU.mult,
                              ALU.mult).then_inc(hsum_step, 1)

            dve.wait_ge(flag_ready, 1)
            usual = dve.value_load(flag[0:1, 0:1], min_val=0, max_val=1)
            with dve.If(usual > 0):
                END = 2 * B + 4

                def add_sums(w, b):
                    dve.wait_ge(partB_ready, w * B + b + 1)
                    dve.scalar_tensor_tensor(both[:, b, :], PA[b % 2][:, 0:2 * C], E[:, 0, bass.ds(w * B + b, 1)],
                                             partB[:, b, :], ALU.mult, ALU.add).then_inc(sums_read, 1)

                def sum_parts(w):
                    e = w * END
                    dve.wait_ge(sums_read, w * B + B + 1)
                    dve.tensor_tensor(num, both[:, :, 0:C], both[:, :, C:2 * C], ALU.add).then_inc(end_step, 1)
                    dve.wait_ge(end_step, e + 1)
                    dve.tensor_scalar(nonei[:, :], num[:, :, D], 0.0, None, ALU.is_equal).then_inc(end_step, 1)
                    dve.wait_ge(end_step, e + 2)
                    for b in range(B):
                        dve.scalar_tensor_tensor(num[:, b, :], meanS[:, :], nonei[:, b:b + 1], num[:, b, :],
                                                 ALU.mult, ALU.add).then_inc(end_step, 1)

                def divide(w):
                    e = w * END
                    dve.wait_ge(end_step, e + 2 + B)
                    dve.reciprocal(rec[:, :], num[:, :, D]).then_inc(end_step, 1)
                    dve.wait_ge(end_step, e + 3 + B)
                    for b in range(B):
                        dve.scalar_tensor_tensor(hp[:, b, :], num[:, b, 0:D], rec[:, b:b + 1], unscale[:, :],
                                                 ALU.mult, ALU.mult).then_inc(end_step, 1)

                def split_sign(w):
                    dve.wait_ge(end_step, w * END + 3 + 2 * B)
                    dve.tensor_scalar(eneg, hp, 0.0, None, ALU.min).then_inc(neg_ready, 1)
                    dve.wait_ge(neg_ready, w + 1)
                    dve.scalar_tensor_tensor(hp, hp, 0.0, x_sb[:, bass.ds(w * B, B), :], ALU.max,
                                             ALU.add).then_inc(end_step, 1)

                def finish(w):
                    dve.wait_ge(end_step, w * END + 4 + 2 * B)
                    dve.wait_ge(eneg_ready, w + 1)
                    dve.wait_ge(res_free, w + 1)
                    dve.scalar_tensor_tensor(res, eneg, -1.0, hp, ALU.add, ALU.add).then_inc(res_ready, 1)

                LAST = 6

                def start_end(b):
                    e = b * LAST
                    dve.wait_ge(sums_read, (G - 1) * B + b + 2)
                    dve.tensor_tensor(num[:, b, :], both[:, b, 0:C], both[:, b, C:2 * C],
                                      ALU.add).then_inc(last_step, 1)
                    dve.wait_ge(last_step, e + 1)
                    dve.tensor_scalar(nonei[:, b:b + 1], num[:, b, D:C], 0.0, None,
                                      ALU.is_equal).then_inc(last_step, 1)
                    dve.wait_ge(last_step, e + 2)
                    dve.scalar_tensor_tensor(num[:, b, :], meanS[:, :], nonei[:, b:b + 1], num[:, b, :],
                                             ALU.mult, ALU.add).then_inc(last_step, 1)
                    dve.wait_ge(last_step, e + 3)
                    dve.reciprocal(rec[:, b:b + 1], num[:, b, D:C]).then_inc(last_step, 1)
                    dve.wait_ge(last_step, e + 4)
                    dve.scalar_tensor_tensor(hp[:, b, :], num[:, b, 0:D], rec[:, b:b + 1], unscale[:, :],
                                             ALU.mult, ALU.mult).then_inc(last_step, 1)
                    dve.wait_ge(last_step, e + 5)
                    dve.wait_ge(res_ready, G - 1)
                    dve.tensor_scalar(eneg[:, b, :], hp[:, b, :], 0.0, None, ALU.min).then_inc(last_neg_ready, 1)
                    dve.wait_ge(last_neg_ready, b + 1)
                    dve.scalar_tensor_tensor(hp[:, b, :], hp[:, b, :], 0.0, x_sb[:, (G - 1) * B + b, :], ALU.max,
                                             ALU.add).then_inc(last_step, 1)

                def finish_end(b):
                    dve.wait_ge(last_step, b * LAST + 6)
                    dve.wait_ge(last_eneg_ready, b + 1)
                    dve.wait_ge(res_free, G)
                    dve.scalar_tensor_tensor(res[:, b, :], eneg[:, b, :], -1.0, hp[:, b, :], ALU.add,
                                             ALU.add).then_inc(last_res_ready, 1)

                def step(w, r, first, last):
                    mask_b(w, r)
                    if not (last and r + 1 == GH):
                        code_edges(w + (r + 1) // GH, (r + 1) % GH, first and r + 1 < R)
                    mask_a(w, r)
                    if not first:
                        if r == 1:
                            add_sums(w - 1, B - 1)
                        if r == 2:
                            sum_parts(w - 1)
                        if r == 3:
                            divide(w - 1)
                        if r == 4:
                            split_sign(w - 1)
                        if r == 5:
                            finish(w - 1)
                    if last and r > 5:
                        finish_end(r - 6)
                    if r % H == 1 and r > 1:
                        add_sums(w, r // H - 1)
                    if last and r >= 5:
                        start_end(r - 5)

                def group(w, first, last, start=0):
                    for r in range(start, GH):
                        step(w, r, first, last)

                dve.wait_ge(exps_ready, 3)
                dve.wait_ge(h_transposed, G)

                def product(w):
                    dve.tensor_tensor(prodA[:, w % 2], Wh[:, slots(w), :], per_slot(F1[:, slots(w)], C),
                                      ALU.mult).then_inc(prodA_ready, 1)

                product(0)
                for w in range(G):
                    if w + 1 < G:
                        if w:
                            dve.wait_ge(ya_ready, w)
                        product(w + 1)
                    if w == 0:
                        dve.wait_ge(mean_done, 1)
                        dve.tensor_copy(meanS[:, 0:D], PMISC[:, 0:D]).then_inc(mean_ready, 1)
                        dve.wait_ge(mean_ready, 1)
                        dve.sem_inc(sums_read, 1)
                    if w in DVE_YB:
                        n = DVE_YB.index(w)
                        dve.tensor_tensor(YB[:, slots(w), 0:C], Wh[:, slots(w), :], per_slot(F2[:, slots(w)], C),
                                          ALU.mult).then_inc(highB_dve_ready, 1)
                        dve.wait_ge(highB_dve_ready, n + 1)
                        for s in range(w * B, (w + 1) * B):
                            dve.scalar_tensor_tensor(YB[:, s, C:2 * C], Wh[:, s, :], F2[:, s:s + 1],
                                                     YB[:, s, 0:C], ALU.mult,
                                                     ALU.subtract).then_inc(yb_dve_ready, 1)
                    dve.wait_ge(highA_ready, w + 1)
                    dve.wait_ge(prodA_ready, w + 1)
                    dve.tensor_tensor(YA[:, slots(w), C:2 * C], prodA[:, w % 2], YA[:, slots(w), 0:C],
                                      ALU.subtract).then_inc(ya_ready, 1)
                    if w == HG - 1:
                        step(0, 1, True, False)
                group(0, True, False, start=2)
                with dve.Fori(1, G - 1) as w:
                    group(w, False, False)
                group(G - 1, False, True)
                finish_end(B - 2)
                add_sums(G - 1, B - 1)
                start_end(B - 1)
                finish_end(B - 1)
            with dve.Else():
                dve.wait_ge(adj_loaded[3], 16)
                for w in range(G):
                    dve.wait_ge(g_row_done, w + 1)
                    dve.tensor_copy(g_s2row[:, w * GC:(w + 1) * GC].rearrange("m (p b) -> m b p", b=B),
                                    PB[w % 2][:, :].rearrange("m (b p) -> m b p", b=B)).then_inc(g_row_stored, 1)
                dve.wait_ge(g_row_stored, G)
                dve.wait_ge(adj_loaded[1], 16)
                dve.wait_ge(adj_loaded[2], 16)

                def general_group(w, first):
                    for b in range(B):
                        k = w * B + b
                        s = bass.ds(w * B + b, 1)
                        g = k * 5
                        if not first or b:
                            dve.wait_ge(g_p_ready, k)
                        dve.tensor_scalar(g_e, g_s2row, s12[:, s, 0], None, ALU.add).then_inc(g_step, 1)
                        dve.wait_ge(g_step, g + 1)
                        dve.scalar_tensor_tensor(g_e, g_e, ALPHA, g_e, ALU.mult, ALU.max).then_inc(g_step, 1)
                        dve.wait_ge(g_loaded, k * 16 + 16)
                        if not first or b:
                            dve.wait_ge(g_transposed, k * G)
                        dve.tensor_scalar(g_m, g_adj, 0.0, -1.0, ALU.is_gt, ALU.add).then_inc(g_step, 1)
                        dve.wait_ge(g_step, g + 3)
                        dve.scalar_tensor_tensor(g_e, g_m, -NEG_INF, g_e, ALU.mult, ALU.add).then_inc(g_step, 1)
                        dve.wait_ge(g_step, g + 4)
                        dve.tensor_reduce(g_nmax[:, :], g_e, AX.X, ALU.max, negate=True).then_inc(g_step, 1)
                        for i in range(G):
                            dve.wait_ge(g_transposed, k * G + i + 1)
                            if i >= 2:
                                dve.wait_ge(g_summed, k * G + i - 1)
                            dve.tensor_copy(g_PT[:, i % 2, :], TP[i % 2][:, :]).then_inc(g_pt_ready, 1)
                        h = k * 5
                        dve.wait_ge(g_summed, k * G + G)
                        dve.tensor_scalar(g_rec[:, :], g_den[:, :], DEN_SCALE, None, ALU.mult).then_inc(g_end_step, 1)
                        dve.wait_ge(g_end_step, h + 1)
                        dve.reciprocal(g_rec[:, :], g_rec[:, :]).then_inc(g_end_step, 1)
                        dve.wait_ge(g_end_step, h + 2)
                        dve.scalar_tensor_tensor(g_hp[:, b, :], PA[0][:, 0:D], g_rec[:, :], unscale[:, :], ALU.mult,
                                                 ALU.mult).then_inc(g_end_step, 1)
                        dve.wait_ge(g_end_step, h + 3)
                        dve.tensor_scalar(eneg[:, b, :], g_hp[:, b, :], 0.0, None, ALU.min).then_inc(g_neg_ready, 1)
                        dve.wait_ge(g_neg_ready, k + 1)
                        dve.tensor_scalar(g_hp[:, b, :], g_hp[:, b, :], 0.0, -1.0, ALU.max,
                                          ALU.add).then_inc(g_end_step, 1)
                        dve.wait_ge(g_end_step, h + 4)
                        dve.tensor_tensor(g_hp[:, b, :], g_hp[:, b, :], x_sb[:, s, :].rearrange("p s d -> p (s d)"),
                                          ALU.add).then_inc(g_end_step, 1)
                        dve.wait_ge(g_end_step, h + 5)
                        dve.wait_ge(g_eneg_ready, k + 1)
                        if b == 0 and not first:
                            dve.wait_ge(g_stored, w * 16)
                        dve.tensor_tensor(res[:, b, :], g_hp[:, b, :], eneg[:, b, :],
                                          ALU.add).then_inc(g_res_ready, 1)

                general_group(0, True)
                with dve.Fori(1, G) as w:
                    general_group(w, False)

        @block.scalar
        def _(act):
            act.dma_start(W_sb[:, :], W[:, :]).then_inc(w_loaded, 16)
            act.dma_start(a_sb[:, 0, :], a1.partition_broadcast(P)).then_inc(a_loaded, 16)
            act.dma_start(a_sb[:, 1, :], a2.partition_broadcast(P)).then_inc(a_loaded, 16)

            def store_hT(w):
                act.wait_ge(h_transposed, w + 1)
                act.activation(hT[:, slots(w), :], TP[w % 2][:, :].rearrange("p (s q) -> p s q", s=B), ACT.Relu,
                               accum_out=hsum[:, w:w + 1]).then_inc(hT_ready, 1)

            def signs(w, first, last):
                for s in range(first, last):
                    act.activation(T8[:, (w + 1) % 2, s, :], s1row[:, bass.ds(w * GC, GC)], ACT.Sign,
                                   bias=s12[:, s, 1:2]).then_inc(signs_ready, 1)

            def first_signs(w):
                act.wait_ge(s12_ready, w + 1)
                if w == 0:
                    act.wait_ge(row_stored, 1)
                signs(0, w * B, (w + 1) * B)

            for w in range(G):
                store_hT(w)
                if w:
                    first_signs(w - 1)
            first_signs(G - 1)
            act.wait_ge(exps_in, 2)
            act.activation(F1[:, :], sF[:, :], ACT.Exp).then_inc(exps_ready, 1)
            act.activation(F2[:, :], sF[:, :], ACT.Exp, scale=ALPHA).then_inc(exps_ready, 1)
            act.wait_ge(exps_in, 4)
            act.activation(E[:, :, :], u08[:, :, :], ACT.Exp).then_inc(exps_ready, 1)

            act.wait_ge(flag_ready, 1)
            usual = act.value_load(flag[0:1, 0:1], min_val=0, max_val=1)
            with act.If(usual > 0):
                for w in range(G):
                    act.wait_ge(prodA_ready, w + 1)
                    act.activation(YA[:, slots(w), 0:C], prodA[:, w % 2], ACT.Copy).then_inc(highA_ready, 1)
                    if w in POOL_YB:
                        n = POOL_YB.index(w)
                        act.wait_ge(prodB_ready, n + 1)
                        act.activation(YB[:, slots(w), 0:C], prodB[:, n % 2], ACT.Copy).then_inc(highB_ready, 1)

                def scale_sums(w, b):
                    act.wait_ge(half_summed, w * GH + H * (b + 1))
                    act.activation(partB[:, b, :], PB[b % 2][:, 0:2 * C], ACT.Copy,
                                   scale=E[:, 1, bass.ds(w * B + b, 1)]).then_inc(partB_ready, 1)

                def end_exp(w):
                    act.wait_ge(neg_ready, w + 1)
                    act.activation(eneg, eneg, ACT.Exp).then_inc(eneg_ready, 1)

                def end_exp_last(b):
                    act.wait_ge(last_neg_ready, b + 1)
                    act.activation(eneg[:, b, :], eneg[:, b, :], ACT.Exp).then_inc(last_eneg_ready, 1)

                def group(w, first, last):
                    q = S // B
                    if not last:
                        if not first:
                            act.wait_ge(bt_ready, w * GH)
                        signs(w + 1, 0, q)
                    for b in range(B):
                        if not last and b < B - 1:
                            signs(w + 1, (b + 1) * q, (b + 2) * q)
                        if b < B - 1:
                            act.wait_ge(sums_read, w * B + 1)
                        scale_sums(w, b)
                        if b == 1 and not first:
                            end_exp(w - 1)
                            if last:
                                end_exp_last(0)
                                end_exp_last(1)
                    if last:
                        end_exp_last(2)
                        end_exp_last(3)

                act.wait_ge(wh_done, G)
                act.wait_ge(mean_done, 1)
                act.wait_ge(row_done, G)
                act.wait_ge(row_stored, G)
                group(0, True, False)
                with act.Fori(1, G - 1) as w:
                    group(w, False, False)
                group(G - 1, False, True)
            with act.Else():
                with act.Fori(0, G) as w:
                    for b in range(B):
                        k = w * B + b
                        act.wait_ge(g_step, k * 5 + 5)
                        act.activation(g_m, g_e, ACT.Exp, bias=g_nmax[:, :],
                                       accum_out=g_den[:, :]).then_inc(g_p_ready, 1)
                        act.wait_ge(g_neg_ready, k + 1)
                        act.activation(eneg[:, b, :], eneg[:, b, :], ACT.Exp).then_inc(g_eneg_ready, 1)

        @block.tensor
        def _(pe):
            pe.wait_ge(consts_set, 5)
            pe.wait_ge(wsq_ready, 1)
            nc.tensor.matmul(PMISC[:, 0:D], ones[:, :], wsq[:, :], start=True, stop=True).then_inc(ssq_done, 1)
            pe.wait_ge(ident_ready, 1)

            def turn_h(w):
                pe.wait_ge(h_ready, (w + 1) * B)
                if w >= 2:
                    pe.wait_ge(hT_ready, w - 1)
                for b in range(B):
                    t = nc.tensor.transpose(TP[w % 2][:, b * P:(b + 1) * P], h_sb[:, w % 2, b, :], ident[:, :])
                t.then_inc(h_transposed, 1)

            def project(w):
                pe.wait_ge(hT_ready, w + 1)
                pe.wait_ge(wext_ready, 3)
                if w >= 2:
                    pe.wait_ge(wh_stored, w - 1)
                    pe.wait_ge(row_stored, w - 1)
                    pe.wait_ge(s12_ready, w - 1)
                if w == 1:
                    pe.wait_ge(scale_step, 1)
                    pe.wait_ge(ok_step, 2)
                for b in range(B):
                    s = w * B + b
                    nc.tensor.matmul(PA[w % 2][:, b * D:(b + 1) * D], hT[:, s, :], Wext[:, 0:D],
                                     start=True, stop=True)
                    t = nc.tensor.matmul(PS12[w % 2][:, 2 * b:2 * b + 2], hT[:, s, :], Wext[:, D:D + 2],
                                         start=True, stop=True)
                t.then_inc(wh_done, 1)
                nc.tensor.matmul(PB[w % 2][:, :], warep[:, 0, :], hT[:, slots(w), :].rearrange("p s q -> p (s q)"),
                                 start=True, stop=True).then_inc(row_done, 1)

            turn_h(0)
            for w in range(G):
                if w + 1 < G:
                    turn_h(w + 1)
                project(w)
            pe.wait_ge(mm_step, 2)
            nc.tensor.transpose(PMISC[0:2, 0:P], mm[:, :], ident[:, :]).then_inc(mm_transposed, 1)
            pe.wait_ge(mm_step, 4)
            nc.tensor.matmul(PMISC[:, 0:2], ones[0:2, :], mmD[:, :], start=True, stop=True).then_inc(mm_spread, 1)
            pe.wait_ge(hsum_step, 2)
            pe.wait_ge(mmB_ready, 1)
            nc.tensor.matmul(PMISC[:, 0:D], hsumrep[:, :], Wext[:, 0:D], start=True, stop=True).then_inc(mean_done, 1)

            pe.wait_ge(flag_ready, 1)
            usual = pe.value_load(flag[0:1, 0:1], min_val=0, max_val=1)
            with pe.If(usual > 0):
                def wait_for_half(w, r):
                    pe.wait_ge(at_ready, w * GH + r + 1)
                    if r % H == 0:
                        pe.wait_ge(sums_read, w * B + r // H)
                    pe.sem_inc(half_started, 1)

                def group(w, last):
                    for r in range(GH):
                        b, hf = r // H, r % H
                        for j in range(HS):
                            s = hf * HS + j
                            if b == 0 and j % B == 0:
                                g = s // B
                                pe.wait_ge(ya_ready, g + 1)
                                if g in DVE_YB:
                                    pe.wait_ge(yb_dve_ready, B * (DVE_YB.index(g) + 1))
                                else:
                                    pe.wait_ge(yb_pool_ready, POOL_YB.index(g) + 1)
                            first, end = s == 0, s == S - 1
                            nc.tensor.matmul(PA[b % 2][:, 0:2 * C], fp8_slot(V, r, j), YA[:, s, :],
                                             start=first, stop=end)
                            t = nc.tensor.matmul(PB[b % 2][:, 0:2 * C], fp8_slot(BT, r, j), YB[:, s, :],
                                                 start=first, stop=end)
                        t.then_inc(half_summed, 1)
                        if not (last and r + 1 == GH):
                            wait_for_half(w + (r + 1) // GH, (r + 1) % GH)

                pe.wait_ge(wh_stored, G)
                pe.wait_ge(row_stored, G)
                pe.wait_ge(at_ready, 1)
                with pe.Fori(0, G - 1) as w:
                    group(w, False)
                group(G - 1, True)
            with pe.Else():
                for w in range(G):
                    pe.wait_ge(row_stored, G)
                    if w >= 2:
                        pe.wait_ge(g_row_stored, w - 1)
                    nc.tensor.matmul(PB[w % 2][:, :], warep[:, 1, :], hT[:, slots(w), :].rearrange(
                        "p s q -> p (s q)"), start=True, stop=True).then_inc(g_row_done, 1)

                def general_group(w, first):
                    for b in range(B):
                        k = w * B + b
                        pe.wait_ge(g_p_ready, k + 1)
                        if not first or b:
                            pe.wait_ge(g_pt_ready, k * G)
                            pe.wait_ge(g_end_step, k * 5)

                        def turn(i):
                            if i >= 2:
                                pe.wait_ge(g_pt_ready, k * G + i - 1)
                            cols = g_m[:, i * GC:(i + 1) * GC].rearrange("i (q c) -> i q c", c=B)
                            for j in range(B):
                                t = nc.tensor.transpose(TP[i % 2][:, j * P:(j + 1) * P], cols[:, :, j], ident[:, :])
                            t.then_inc(g_transposed, 1)

                        turn(0)
                        for i in range(G):
                            if i + 1 < G:
                                turn(i + 1)
                            pe.wait_ge(g_pt_ready, k * G + i + 1)
                            for j in range(B):
                                t = nc.tensor.matmul(PA[0][:, 0:D], g_PT[:, i % 2, j * P:(j + 1) * P],
                                                     Wh[:, i * B + j, 0:D], start=(i == 0 and j == 0),
                                                     stop=(i == G - 1 and j == B - 1))
                            t.then_inc(g_summed, 1)

                pe.wait_ge(wh_stored, G)
                general_group(0, True)
                with pe.Fori(1, G) as w:
                    general_group(w, False)


def kernel(x, adj, L0_gnn_W, L0_gnn_a1, L0_gnn_a2):
    import numpy as np
    import concourse.bacc as bacc
    from concourse import mybir
    from concourse.bass_utils import run_bass_kernel_spmd

    nc = bacc.Bacc("TRN2", target_bir_lowering=False, num_devices=1)
    arrays, args = {}, []
    n, p, b = x.shape[0], 128, 4
    adjT = np.asarray(adj).reshape(n // (p * b), p, b, n // (p * b), p, b).transpose(0, 2, 4, 3, 5, 1).reshape(
        n // (p * b), b, p, n)
    for name, a in (("x", x), ("adj", adj), ("adjT", adjT), ("W", L0_gnn_W), ("a1", L0_gnn_a1), ("a2", L0_gnn_a2)):
        a = np.ascontiguousarray(a)
        arrays[f"in_{name}"] = a
        args.append(nc.dram_tensor(f"in_{name}", a.shape, mybir.dt.from_np(a.dtype), kind="ExternalInput").ap())
    out = nc.dram_tensor("out", x.shape, mybir.dt.float32, kind="ExternalOutput").ap()
    build(nc, *args, out)
    r = run_bass_kernel_spmd(nc, [arrays], core_ids=[0])
    return r.results[0]["out"]
```

```python
import concourse.bass as bass
from concourse import mybir
from contextlib import ExitStack


def build(nc, x, adj, adjT, W, a1, a2, out):
    f32, i32 = mybir.dt.float32, mybir.dt.int32
    f16, u8, i8, fp8 = mybir.dt.float16, mybir.dt.uint8, mybir.dt.int8, mybir.dt.float8e4
    ALU = mybir.AluOpType
    ACT = mybir.ActivationFunctionType
    AX = mybir.AxisListType

    N, D = x.shape
    P = 128
    B = 4
    G = N // (P * B)
    S = G * B
    GC = P * B
    H = 2
    HC = N // H
    HS = S // H
    GH = B * H
    C = D + 1
    TILES = B
    R = 4
    ORDER = [(b, hf) for b in range(B) for hf in range(H)]
    FIRST_ORDER = [(0, 0), (1, 0), (0, 1), (1, 1)] + ORDER[4:]
    ALPHA = 0.2
    NEG_INF = -9000000000000000.0
    EPS = 1e-5
    SPREAD = 8.0
    EDGE = 8
    DEN_SCALE = 2.0 ** 14
    EXP_ONE = 2.0 ** 23
    SCALE_EXP = 127 + 11 - (64 - 127)
    UNSCALE_EXP = 127 + 14 + (64 - 127) - 11
    HALF_EXP_MIN, HALF_EXP_MAX = 2.0 ** (14 - 127), 2.0 ** (112 - 127)
    DVE_NORM = [B if w < 2 else B - 1 if w < 4 else B - 2 for w in range(G)]
    ACT_YA = 5
    DVE_YB = (5,)
    POOL_YB = tuple(g for g in range(G) if g not in DVE_YB)

    x_v = x.rearrange("(w p b) d -> p w (b d)", p=P, b=B)
    out_v = out.rearrange("(w p b) d -> w p (b d)", p=P, b=B)
    adj_v = adj.rearrange("(w p b) j -> w b p j", p=P, b=B)

    ctx = ExitStack()
    with ctx:
        def sb(name, shape, dt):
            return ctx.enter_context(nc.sbuf_tensor(name, shape, dt))

        def sem(name):
            return ctx.enter_context(nc.semaphore(name))

        x_sb = sb("x_sb", [P, S, D], f32)
        T_mem = sb("T_mem", [P, 2 * N], f32)
        hT = T_mem[:, 0:N].rearrange("p (s q) -> p s q", q=P)
        T8 = T_mem[:, :].bitcast(i8).rearrange("p (r s i) -> p r s i", r=2, s=S)
        T32 = T_mem[:, :].bitcast(i32).rearrange("p (r s q) -> p r s q", r=2, s=S)
        s1row = sb("s1row", [P, N], f32)
        WhM = sb("WhM", [P, S * C], f32)
        Wh = WhM[:, :].rearrange("p (s c) -> p s c", c=C)
        partB = WhM[:, 0:B * 2 * C].rearrange("p (s c) -> p s c", s=B)
        both = WhM[:, B * 2 * C:2 * B * 2 * C].rearrange("p (s c) -> p s c", s=B)
        num = WhM[:, 4 * B * C:5 * B * C].rearrange("p (s c) -> p s c", s=B)
        hp = WhM[:, 5 * B * C:5 * B * C + B * D].rearrange("p (s d) -> p s d", s=B)
        YA = sb("YA", [P, S, 2 * C], f16)
        YB = sb("YB", [P, S, 2 * C], f16)
        adj_sb = sb("adj_sb", [P, TILES, N], i32)
        V = sb("V", [P, R, HC], u8)
        BT = sb("BT", [P, R, HC], u8)
        early = BT[:, R - 2:R, :].rearrange("p r c -> p (r c)").bitcast(f32)
        W_sb = early[:, 0:D]
        wsq = early[:, D:2 * D]
        expo = early[:, 2 * D:3 * D].bitcast(i32)
        scale = early[:, 3 * D:4 * D].bitcast(i32)
        a_sb = early[:, 4 * D:6 * D].rearrange("p (a d) -> p a d", a=2)
        scratch = sb("scratch", [P, 4 * B * C], f32)
        h_sb = scratch[:, 0:2 * GC].rearrange("p (r s d) -> p r s d", r=2, s=B)
        prodA = scratch[:, 0:2 * B * C].rearrange("p (r s c) -> p r s c", r=2, s=B)
        prodB = scratch[:, 2 * B * C:4 * B * C].rearrange("p (r s c) -> p r s c", r=2, s=B)
        eneg = scratch[:, 0:GC].rearrange("p (s d) -> p s d", s=B)
        res = scratch[:, GC:2 * GC].rearrange("p (s d) -> p s d", s=B)
        ident = sb("ident", [P, P], f32)
        ones = sb("ones", [P, P], f32)
        Wext = sb("Wext", [P, D + 2], f32)
        warep = sb("warep", [P, 2, P], f32)
        unscale = sb("unscale", [P, D], f32)
        minushalf = sb("minushalf", [P, S], f32)
        stats = sb("stats", [P, S, 6], f32)
        mv = sb("mv", [P, S, 2], f32)
        veps = sb("veps", [P, S], f32)
        rstd = sb("rstd", [P, S], f32)
        hsum = sb("hsum", [P, G], f32)
        hsum1 = sb("hsum1", [P, 1], f32)
        hsumrep = sb("hsumrep", [P, P], f32)
        meanS = sb("meanS", [P, C], f32)
        s12 = sb("s12", [P, S, 2], f32)
        mm = sb("mm", [P, 2], f32)
        mmT = sb("mmT", [2, 1], f32)
        mmD = sb("mmD", [2, 2], f32)
        mmB = sb("mmB", [P, 2], f32)
        sF = sb("sF", [P, S], f32)
        u08 = sb("u08", [P, 2, S], f32)
        F1 = sb("F1", [P, S], f32)
        F2 = sb("F2", [P, S], f32)
        E = sb("E", [P, 2, S], f32)
        exp_lim = sb("exp_lim", [P, 2], f32)
        ok = sb("ok", [P, 4], f32)
        flag = sb("flag", [P, 1], i32)
        nonei = sb("nonei", [P, B], f32)
        rec = sb("rec", [P, B], f32)
        g_adj = adj_sb[:, 0, :]
        g_e = adj_sb[:, 1, :].bitcast(f32)
        g_m = adj_sb[:, 2, :].bitcast(f32)
        g_s2row = adj_sb[:, 3, :].bitcast(f32)
        g_PT = YA[:, :, :].rearrange("p s c -> p (s c)")[:, 0:4 * GC].bitcast(f32).rearrange(
            "p (r c) -> p r c", r=2)
        g_hp = scratch[:, 2 * GC:3 * GC].rearrange("p (s d) -> p s d", s=B)
        g_nmax = sb("g_nmax", [P, 1], f32)
        g_den = sb("g_den", [P, 1], f32)
        g_rec = sb("g_rec", [P, 1], f32)

        def bank(name):
            return ctx.enter_context(nc.psum_tensor(name, [P, 512], f32))

        TP = [bank("TP0"), bank("TP1")]
        PB = [bank("PB0"), bank("PB1")]
        PW = ctx.enter_context(nc.psum_tensor("PW", [P, 2 * H, 512], f32))
        PA = [PW[:, 0, :], PW[:, 1, :]]
        PMISC = PW[:, 3, :]

        def projected(w):
            return PW[:, w % 2 * H:(w % 2 + 1) * H, 0:B // H * (D + 2)].rearrange("p h (s c) -> p h s c", s=B // H)

        x_loaded = [sem(f"x_loaded{w}") for w in range(G)]
        w_loaded = sem("w_loaded")
        a_loaded = sem("a_loaded")
        adj_loaded = [sem(f"adj_loaded{i}") for i in range(TILES)]
        consts_set = sem("consts_set")
        ident_ready = sem("ident_ready")
        wsq_ready = sem("wsq_ready")
        ssq_done = sem("ssq_done")
        scale_step = sem("scale_step")
        wa_step = sem("wa_step")
        wext_ready = sem("wext_ready")
        stats_done = sem("stats_done")
        mv_done = sem("mv_done")
        veps_ready = sem("veps_ready")
        rstd_ready = sem("rstd_ready")
        h_dve_ready = sem("h_dve_ready")
        h_pool_ready = sem("h_pool_ready")
        h_transposed = sem("h_transposed")
        hT_ready = sem("hT_ready")
        wh_done = sem("wh_done")
        wh_stored = sem("wh_stored")
        row_done = sem("row_done")
        row_stored = [sem("row_stored0"), sem("row_stored1")]
        hsum_step = sem("hsum_step")
        mean_done = sem("mean_done")
        mean_ready = sem("mean_ready")
        s12_ready = sem("s12_ready")
        mm_step = sem("mm_step")
        mm_transposed = sem("mm_transposed")
        mm_spread = sem("mm_spread")
        mmB_ready = sem("mmB_ready")
        exps_in = sem("exps_in")
        exps_ready = sem("exps_ready")
        ok_step = sem("ok_step")
        flag_ready = sem("flag_ready")
        prodA_ready = sem("prodA_ready")
        prodB_ready = sem("prodB_ready")
        highA_ready = sem("highA_ready")
        highB_ready = sem("highB_ready")
        ya_ready = sem("ya_ready")
        yb_pool_ready = sem("yb_pool_ready")
        highA_act_ready = sem("highA_act_ready")
        highB_act_ready = sem("highB_act_ready")
        ya_low_ready = sem("ya_low_ready")
        yb_dve_ready = sem("yb_dve_ready")
        signs_ready = sem("signs_ready")
        v_ready = sem("v_ready")
        bt_ready = sem("bt_ready")
        at_ready = sem("at_ready")
        half_started = sem("half_started")
        last_b_summed = sem("last_b_summed")
        half_summed = sem("half_summed")
        partB_ready = sem("partB_ready")
        end_step = sem("end_step")
        sums_read = sem("sums_read")
        neg_ready = sem("neg_ready")
        eneg_ready = sem("eneg_ready")
        res_ready = sem("res_ready")
        out_stored = sem("out_stored")
        res_free = sem("res_free")
        last_step = sem("last_step")
        last_neg_ready = sem("last_neg_ready")
        last_eneg_ready = sem("last_eneg_ready")
        last_res_ready = sem("last_res_ready")
        last_stored = sem("last_stored")
        g_row_done = sem("g_row_done")
        g_row_stored = sem("g_row_stored")
        g_loaded = sem("g_loaded")
        g_step = sem("g_step")
        g_p_ready = sem("g_p_ready")
        g_transposed = sem("g_transposed")
        g_pt_ready = sem("g_pt_ready")
        g_summed = sem("g_summed")
        g_end_step = sem("g_end_step")
        g_neg_ready = sem("g_neg_ready")
        g_eneg_ready = sem("g_eneg_ready")
        g_res_ready = sem("g_res_ready")
        g_stored = sem("g_stored")

        def slots(w):
            return slice(w * B, (w + 1) * B)

        def part(w, r):
            return (FIRST_ORDER if isinstance(w, int) and w == 0 else ORDER)[r]

        def per_slot(a, n):
            return a.unsqueeze(2).to_broadcast([P, B, n])

        def half_words(m, r):
            return m[:, r % R, :].bitcast(i32).rearrange("p (s q) -> p s q", s=HS)

        def fp8_slot(m, r, j):
            return m[:, r % R, j * P:(j + 1) * P].bitcast(fp8)

        def normalise(engine, w, first, last, ready):
            engine.wait_ge(rstd_ready, w + 1)
            if w >= 2:
                engine.wait_ge(h_transposed, w - 1)
            for b in range(first, last):
                s = w * B + b
                engine.tensor_scalar(h_sb[:, w % 2, b, :], x_sb[:, s, :], mv[:, s, 0:1], rstd[:, s:s + 1],
                                     ALU.subtract, ALU.mult).then_inc(ready, 1)

        block = ctx.enter_context(nc.Block())

        @block.sync
        def _(sp):
            for w in range(G):
                sp.dma_start(x_sb[:, slots(w), :].rearrange("p b d -> p (b d)"), x_v[:, w, :]).then_inc(x_loaded[w], 16)
            for t in range(TILES):
                sp.dma_start(adj_sb[:, t, :], adjT[0, t]).then_inc(adj_loaded[t], 16)
            sp.wait_ge(flag_ready, 1)
            usual = sp.value_load(flag[0:1, 0:1], min_val=0, max_val=1)
            with sp.If(usual > 0):
                def load_tile(w, b, coded):
                    sp.wait_ge(v_ready, coded)
                    sp.dma_start(adj_sb[:, b, :], adjT[w, b]).then_inc(adj_loaded[b], 16)

                for b in range(B):
                    load_tile(1, b, max(FIRST_ORDER.index((b, hf)) for hf in range(H)) + 1)
                with sp.Fori(2, G) as w:
                    for b in range(B):
                        load_tile(w, b, w * GH - GH + H * (b + 1))
                for b in range(B):
                    sp.wait_ge(last_res_ready, b + 1)
                    sp.dma_start(out_v[G - 1][:, b * D:(b + 1) * D], res[:, b, :]).then_inc(last_stored, 16)
                sp.wait_ge(last_stored, 16 * B)
            with sp.Else():
                sp.wait_ge(v_ready, R)
                for t in range(TILES):
                    sp.wait_ge(adj_loaded[t], 16)

                def general_group(w, first):
                    for b in range(B):
                        if not first or b:
                            sp.wait_ge(g_step, w * (B * 5) + b * 5)
                        sp.dma_start(g_adj, adj_v[w, b]).then_inc(g_loaded, 16)
                    sp.wait_ge(g_res_ready, w * B + B)
                    sp.dma_start(out_v[w], res.rearrange("p s d -> p (s d)")).then_inc(g_stored, 16)

                general_group(0, True)
                with sp.Fori(1, G) as w:
                    general_group(w, False)
                sp.wait_ge(g_stored, 16 * G)

        @block.gpsimd
        def _(pool):
            pool.memset(ones[:, :], 1.0).then_inc(consts_set, 1)
            pool.memset(minushalf[:, :], -0.5).then_inc(consts_set, 1)
            pool.memset(Wh[:, :, D:C], DEN_SCALE).then_inc(consts_set, 1)
            pool.memset(meanS[:, D:C], DEN_SCALE).then_inc(consts_set, 1)
            pool.memset(ident[:, :], 0.0).then_inc(consts_set, 1)
            pool.wait_ge(consts_set, 5)
            pool.affine_select(out=ident[:, :], in_=ident[:, :], compare_op=ALU.not_equal, fill=1.0,
                               base=0, pattern=[[-1, P]], channel_multiplier=1).then_inc(ident_ready, 1)
            for w in range(G):
                pool.wait_ge(veps_ready, w + 1)
                pool.tensor_tensor(rstd[:, slots(w)], veps[:, slots(w)], minushalf[:, slots(w)],
                                   ALU.pow).then_inc(rstd_ready, 1)
                if DVE_NORM[w] < B:
                    normalise(pool, w, DVE_NORM[w], B, h_pool_ready)
            pool.wait_ge(exps_ready, 2)
            pool.wait_ge(wh_stored, G)
            pool.wait_ge(h_transposed, G)

            def product(n):
                pool.tensor_tensor(prodB[:, n % 2], Wh[:, slots(POOL_YB[n]), :],
                                   per_slot(F2[:, slots(POOL_YB[n])], C), ALU.mult).then_inc(prodB_ready, 1)

            product(0)
            for n, w in enumerate(POOL_YB):
                if n + 1 < len(POOL_YB):
                    if n:
                        pool.wait_ge(yb_pool_ready, n)
                    product(n + 1)
                pool.wait_ge(highB_ready, n + 1)
                pool.wait_ge(prodB_ready, n + 1)
                pool.tensor_tensor(YB[:, slots(w), C:2 * C], prodB[:, n % 2], YB[:, slots(w), 0:C],
                                   ALU.subtract).then_inc(yb_pool_ready, 1)
            pool.wait_ge(flag_ready, 1)
            usual = pool.value_load(flag[0:1, 0:1], min_val=0, max_val=1)
            with pool.If(usual > 0):
                pool.sem_inc(res_free, 1)
                with pool.Fori(0, G - 1) as w:
                    pool.wait_ge(res_ready, w + 1)
                    pool.dma_start(out_v[w], res.rearrange("p s d -> p (s d)")).then_inc(out_stored, 16)
                    pool.wait_ge(out_stored, w * 16 + 16)
                    pool.sem_inc(res_free, 1)

        @block.vector
        def _(dve):
            def row_stats(w):
                dve.wait_ge(x_loaded[w], 16)
                for s in range(w * B, (w + 1) * B):
                    dve.bn_stats(stats[:, s, :], x_sb[:, s, :]).then_inc(stats_done, 1)
                for s in range(w * B, (w + 1) * B):
                    dve.wait_ge(stats_done, s + 1)
                    dve.bn_aggr(mv[:, s, :], stats[:, s, :]).then_inc(mv_done, 1)
                dve.wait_ge(mv_done, (w + 1) * B)
                dve.tensor_scalar(veps[:, slots(w)], mv[:, slots(w), 1], EPS, None, ALU.add).then_inc(veps_ready, 1)

            row_stats(0)
            row_stats(1)
            dve.wait_ge(w_loaded, 16)
            dve.wait_ge(a_loaded, 32)
            dve.wait_ge(consts_set, 5)
            for a in range(2):
                if a:
                    dve.wait_ge(wa_step, 2)
                dve.tensor_tensor(hsumrep[:, :], W_sb[:, :], a_sb[:, a, :], ALU.mult).then_inc(wa_step, 1)
                dve.wait_ge(wa_step, 2 * a + 1)
                dve.tensor_reduce(Wext[:, D + a:D + a + 1], hsumrep[:, :], AX.X, ALU.add).then_inc(wa_step, 1)
            normalise(dve, 0, 0, DVE_NORM[0], h_dve_ready)
            dve.wait_ge(ssq_done, 1)
            dve.tensor_scalar(expo[:, :], PMISC[:, 0:D].bitcast(i32), 24, 23, ALU.logical_shift_right,
                              ALU.logical_shift_left).then_inc(scale_step, 1)
            dve.wait_ge(scale_step, 1)
            dve.tensor_scalar(scale[:, :], expo[:, :], -1.0, SCALE_EXP * EXP_ONE, ALU.mult,
                              ALU.add).then_inc(scale_step, 1)
            dve.tensor_scalar(unscale[:, :].bitcast(i32), expo[:, :], UNSCALE_EXP * EXP_ONE, None,
                              ALU.add).then_inc(scale_step, 1)
            dve.wait_ge(scale_step, 3)
            dve.tensor_tensor(Wext[:, 0:D], W_sb[:, :], scale[:, :].bitcast(f32), ALU.mult).then_inc(wext_ready, 1)

            def code_edges(w, r, early):
                b, hf = part(w, r)
                dve.wait_ge(adj_loaded[b], w * 16 + 16)
                if not early:
                    dve.wait_ge(half_summed, w * GH + r - R + 1)
                dve.tensor_scalar(V[:, r % R, :], adj_sb[:, b, hf * HC:(hf + 1) * HC], 0.0, float(EDGE),
                                  ALU.is_gt, ALU.mult).then_inc(v_ready, 1)

            def mask_b(w, r):
                b, hf = part(w, r)
                dve.wait_ge(v_ready, w * GH + r + 1)
                dve.wait_ge(signs_ready, w * S + (hf + 1) * HS)
                signs = T32[:, (w + 1) % 2, hf * HS:(hf + 1) * HS, b * P // B:(b + 1) * P // B]
                dve.tensor_tensor(half_words(BT, r), half_words(V, r), signs, ALU.bitwise_and).then_inc(bt_ready, 1)

            def mask_a(w, r):
                dve.wait_ge(bt_ready, w * GH + r + 1)
                dve.tensor_tensor(half_words(V, r), half_words(V, r), half_words(BT, r),
                                  ALU.bitwise_xor).then_inc(at_ready, 1)

            def ahead(w):
                if w + 3 < G:
                    row_stats(w + 3)
                if w + 2 < G:
                    normalise(dve, w + 2, 0, DVE_NORM[w + 2], h_dve_ready)

            normalise(dve, 1, 0, DVE_NORM[1], h_dve_ready)
            row_stats(2)
            for w in range(G):
                if w:
                    ahead(w)
                dve.wait_ge(wh_done, w + 1)
                dve.tensor_copy(s12[:, slots(w), :].rearrange("p (h s) a -> p h s a", h=H),
                                projected(w)[:, :, :, D:D + 2]).then_inc(s12_ready, 1)
                dve.tensor_copy(Wh[:, slots(w), 0:D].rearrange("p (h s) d -> p h s d", h=H),
                                projected(w)[:, :, :, 0:D]).then_inc(wh_stored, 1)
                if w == 0:
                    ahead(w)
                if w % 2:
                    dve.wait_ge(row_done, w + 1)
                    dve.tensor_copy(s1row[:, w * GC:(w + 1) * GC], PB[w % 2][:, :]).then_inc(row_stored[1], 1)
                if w == G - 3:
                    code_edges(0, 0, True)
            dve.wait_ge(s12_ready, G)
            dve.tensor_reduce(mm[:, 0:1], s12[:, :, 1], AX.X, ALU.max).then_inc(mm_step, 1)
            dve.tensor_reduce(mm[:, 1:2], s12[:, :, 1], AX.X, ALU.min, negate=True).then_inc(mm_step, 1)
            mask_b(0, 0)
            dve.wait_ge(mm_transposed, 1)
            dve.tensor_reduce(mmT[:, :], PMISC[0:2, 0:P], AX.X, ALU.max).then_inc(mm_step, 1)
            dve.wait_ge(mm_step, 3)
            dve.tensor_scalar(mmD[:, :], ident[0:2, 0:2], mmT[:, :], None, ALU.mult).then_inc(mm_step, 1)
            mask_a(0, 0)
            dve.wait_ge(mm_spread, 1)
            dve.tensor_copy(mmB[:, :], PMISC[:, 0:2]).then_inc(mmB_ready, 1)
            dve.wait_ge(mmB_ready, 1)
            dve.tensor_scalar(sF[:, :], s12[:, :, 1], mmB[:, 0:1], None, ALU.subtract).then_inc(exps_in, 1)
            dve.tensor_scalar(u08[:, 0, :], s12[:, :, 0], mmB[:, 0:1], 1.0 - ALPHA, ALU.add,
                              ALU.mult).then_inc(exps_in, 1)
            dve.wait_ge(exps_in, 2)
            dve.tensor_scalar(u08[:, 1, :], u08[:, 0, :], -1.0, 0.0, ALU.mult, ALU.min).then_inc(exps_in, 1)
            dve.wait_ge(exps_in, 3)
            dve.tensor_scalar(u08[:, 0, :], u08[:, 0, :], 0.0, None, ALU.min).then_inc(exps_in, 1)
            dve.wait_ge(hT_ready, G)
            dve.tensor_reduce(hsum1[:, :], hsum[:, :], AX.X, ALU.add).then_inc(hsum_step, 1)
            dve.wait_ge(hsum_step, 1)
            dve.tensor_scalar(hsumrep[:, :], ones[:, :], hsum1[:, :], 1.0 / N, ALU.mult,
                              ALU.mult).then_inc(hsum_step, 1)

            def choose_path():
                for a, extreme in enumerate((ALU.min, ALU.max)):
                    dve.tensor_reduce(exp_lim[:, a:a + 1], expo.bitcast(f32), AX.X, extreme).then_inc(ok_step, 1)
                dve.tensor_tensor(ok[:, 0:1], mmB[:, 0:1], mmB[:, 1:2], ALU.add).then_inc(ok_step, 1)
                dve.wait_ge(ok_step, 3)
                dve.tensor_scalar(ok[:, 1:2], ok[:, 0:1], SPREAD, None, ALU.is_le).then_inc(ok_step, 1)
                dve.wait_ge(ok_step, 4)
                dve.scalar_tensor_tensor(ok[:, 2:3], exp_lim[:, 0:1], HALF_EXP_MIN, ok[:, 1:2], ALU.is_ge,
                                         ALU.mult).then_inc(ok_step, 1)
                dve.wait_ge(ok_step, 5)
                dve.scalar_tensor_tensor(flag[:, :], exp_lim[:, 1:2], HALF_EXP_MAX, ok[:, 2:3], ALU.is_le,
                                         ALU.mult).then_inc(flag_ready, 1)

            dve.wait_ge(exps_ready, 1)
            dve.wait_ge(h_transposed, G)

            def product(w):
                dve.tensor_tensor(prodA[:, w % 2], Wh[:, slots(w), :], per_slot(F1[:, slots(w)], C),
                                  ALU.mult).then_inc(prodA_ready, 1)

            MASKS_AFTER = (2, 4)
            product(0)
            for w in range(G):
                if w + 1 < ACT_YA:
                    if w:
                        dve.wait_ge(ya_ready, w)
                    product(w + 1)
                if w == 0:
                    choose_path()
                if w in DVE_YB:
                    n = DVE_YB.index(w)
                    dve.wait_ge(highB_act_ready, B * (n + 1))
                    for s in range(w * B, (w + 1) * B):
                        dve.scalar_tensor_tensor(YB[:, s, C:2 * C], Wh[:, s, :], F2[:, s:s + 1],
                                                 YB[:, s, 0:C], ALU.mult,
                                                 ALU.subtract).then_inc(yb_dve_ready, 1)
                if w < ACT_YA:
                    dve.wait_ge(highA_ready, w + 1)
                    dve.wait_ge(prodA_ready, w + 1)
                    dve.tensor_tensor(YA[:, slots(w), C:2 * C], prodA[:, w % 2], YA[:, slots(w), 0:C],
                                      ALU.subtract).then_inc(ya_ready, 1)
                else:
                    for s in range(w * B, (w + 1) * B):
                        dve.wait_ge(highA_act_ready, s - ACT_YA * B + 1)
                        dve.scalar_tensor_tensor(YA[:, s, C:2 * C], Wh[:, s, :], F1[:, s:s + 1], YA[:, s, 0:C],
                                                 ALU.mult, ALU.subtract).then_inc(ya_low_ready, 1)
                if w == 0:
                    code_edges(0, 1, True)
                if w in MASKS_AFTER:
                    r = MASKS_AFTER.index(w) + 1
                    mask_b(0, r)
                    code_edges(0, r + 1, True)
                    mask_a(0, r)

            dve.wait_ge(flag_ready, 1)
            usual = dve.value_load(flag[0:1, 0:1], min_val=0, max_val=1)
            with dve.If(usual > 0):
                END = 2 * B + 4

                def add_sums(w, b, final=False):
                    if final:
                        dve.wait_ge(half_summed, G * GH)
                    dve.wait_ge(partB_ready, w * B + b + 1)
                    dve.scalar_tensor_tensor(both[:, b, :], PA[b % 2][:, 0:2 * C], E[:, 0, bass.ds(w * B + b, 1)],
                                             partB[:, b, :], ALU.mult, ALU.add).then_inc(sums_read, 1)

                def sum_parts(w):
                    e = w * END
                    dve.wait_ge(sums_read, w * B + B + 1)
                    dve.tensor_tensor(num, both[:, :, 0:C], both[:, :, C:2 * C], ALU.add).then_inc(end_step, 1)
                    dve.wait_ge(end_step, e + 1)
                    dve.tensor_scalar(nonei[:, :], num[:, :, D], 0.0, None, ALU.is_equal).then_inc(end_step, 1)
                    dve.wait_ge(end_step, e + 2)
                    for b in range(B):
                        dve.scalar_tensor_tensor(num[:, b, :], meanS[:, :], nonei[:, b:b + 1], num[:, b, :],
                                                 ALU.mult, ALU.add).then_inc(end_step, 1)

                def divide(w):
                    e = w * END
                    dve.wait_ge(end_step, e + 2 + B)
                    dve.reciprocal(rec[:, :], num[:, :, D]).then_inc(end_step, 1)
                    dve.wait_ge(end_step, e + 3 + B)
                    for b in range(B):
                        dve.scalar_tensor_tensor(hp[:, b, :], num[:, b, 0:D], rec[:, b:b + 1], unscale[:, :],
                                                 ALU.mult, ALU.mult).then_inc(end_step, 1)

                def split_sign(w):
                    dve.wait_ge(end_step, w * END + 3 + 2 * B)
                    dve.tensor_scalar(eneg, hp, 0.0, None, ALU.min).then_inc(neg_ready, 1)
                    dve.wait_ge(neg_ready, w + 1)
                    dve.scalar_tensor_tensor(hp, hp, 0.0, x_sb[:, bass.ds(w * B, B), :], ALU.max,
                                             ALU.add).then_inc(end_step, 1)

                def finish(w):
                    dve.wait_ge(end_step, w * END + 4 + 2 * B)
                    dve.wait_ge(eneg_ready, w + 1)
                    dve.wait_ge(res_free, w + 1)
                    dve.scalar_tensor_tensor(res, eneg, -1.0, hp, ALU.add, ALU.add).then_inc(res_ready, 1)

                LAST = 6

                def start_end(b):
                    e = b * LAST
                    dve.wait_ge(sums_read, (G - 1) * B + b + 2)
                    dve.tensor_tensor(num[:, b, :], both[:, b, 0:C], both[:, b, C:2 * C],
                                      ALU.add).then_inc(last_step, 1)
                    dve.wait_ge(last_step, e + 1)
                    dve.tensor_scalar(nonei[:, b:b + 1], num[:, b, D:C], 0.0, None,
                                      ALU.is_equal).then_inc(last_step, 1)
                    dve.wait_ge(last_step, e + 2)
                    dve.scalar_tensor_tensor(num[:, b, :], meanS[:, :], nonei[:, b:b + 1], num[:, b, :],
                                             ALU.mult, ALU.add).then_inc(last_step, 1)
                    dve.wait_ge(last_step, e + 3)
                    dve.reciprocal(rec[:, b:b + 1], num[:, b, D:C]).then_inc(last_step, 1)
                    dve.wait_ge(last_step, e + 4)
                    dve.scalar_tensor_tensor(hp[:, b, :], num[:, b, 0:D], rec[:, b:b + 1], unscale[:, :],
                                             ALU.mult, ALU.mult).then_inc(last_step, 1)
                    dve.wait_ge(last_step, e + 5)
                    dve.wait_ge(res_ready, G - 1)
                    dve.tensor_scalar(eneg[:, b, :], hp[:, b, :], 0.0, None, ALU.min).then_inc(last_neg_ready, 1)
                    dve.wait_ge(last_neg_ready, b + 1)
                    dve.scalar_tensor_tensor(hp[:, b, :], hp[:, b, :], 0.0, x_sb[:, (G - 1) * B + b, :], ALU.max,
                                             ALU.add).then_inc(last_step, 1)

                def finish_end(b):
                    dve.wait_ge(last_step, b * LAST + 6)
                    dve.wait_ge(last_eneg_ready, b + 1)
                    dve.wait_ge(res_free, G)
                    dve.scalar_tensor_tensor(res[:, b, :], eneg[:, b, :], -1.0, hp[:, b, :], ALU.add,
                                             ALU.add).then_inc(last_res_ready, 1)

                def step(w, r, first, last):
                    mask_b(w, r)
                    if not (last and r + 1 == GH):
                        code_edges(w + (r + 1) // GH, (r + 1) % GH, first and r + 1 < R)
                    mask_a(w, r)
                    if not first:
                        if r in (0, 2):
                            add_sums(w - 1, r // 2 + 2)
                        if r == 3:
                            sum_parts(w - 1)
                    if r in (4, 6):
                        add_sums(w, r // 2 - 2)
                    if last:
                        if r == 4:
                            divide(w - 1)
                            split_sign(w - 1)
                        if r == 5:
                            finish(w - 1)
                            start_end(0)
                        if r == 6:
                            finish_end(0)
                            start_end(1)
                        if r == 7:
                            finish_end(1)
                    elif not first:
                        if r == 5:
                            divide(w - 1)
                        if r == 6:
                            split_sign(w - 1)
                        if r == 7:
                            finish(w - 1)

                def group(w, first, last, start=0):
                    for r in range(start, GH):
                        step(w, r, first, last)

                dve.sem_inc(sums_read, 1)
                step(0, 3, True, False)
                dve.wait_ge(mean_done, 1)
                dve.tensor_copy(meanS[:, 0:D], PMISC[:, 0:D]).then_inc(mean_ready, 1)
                dve.wait_ge(mean_ready, 1)
                dve.wait_ge(exps_ready, 3)
                group(0, True, False, start=4)
                with dve.Fori(1, G - 1) as w:
                    group(w, False, False)
                group(G - 1, False, True)
                for b in range(2, B):
                    add_sums(G - 1, b, b == B - 1)
                    start_end(b)
                    finish_end(b)
            with dve.Else():
                dve.wait_ge(adj_loaded[3], 16)
                for w in range(G):
                    dve.wait_ge(g_row_done, w + 1)
                    dve.tensor_copy(g_s2row[:, w * GC:(w + 1) * GC].rearrange("m (p b) -> m b p", b=B),
                                    PB[w % 2][:, :].rearrange("m (b p) -> m b p", b=B)).then_inc(g_row_stored, 1)
                dve.wait_ge(g_row_stored, G)
                dve.wait_ge(adj_loaded[1], 16)
                dve.wait_ge(adj_loaded[2], 16)
                dve.wait_ge(highA_ready, ACT_YA)
                dve.wait_ge(highA_act_ready, (G - ACT_YA) * B)
                dve.wait_ge(yb_pool_ready, len(POOL_YB))

                def general_group(w, first):
                    for b in range(B):
                        k = w * B + b
                        s = bass.ds(w * B + b, 1)
                        g = k * 5
                        if not first or b:
                            dve.wait_ge(g_p_ready, k)
                        dve.tensor_scalar(g_e, g_s2row, s12[:, s, 0], None, ALU.add).then_inc(g_step, 1)
                        dve.wait_ge(g_step, g + 1)
                        dve.scalar_tensor_tensor(g_e, g_e, ALPHA, g_e, ALU.mult, ALU.max).then_inc(g_step, 1)
                        dve.wait_ge(g_loaded, k * 16 + 16)
                        if not first or b:
                            dve.wait_ge(g_transposed, k * G)
                        dve.tensor_scalar(g_m, g_adj, 0.0, -1.0, ALU.is_gt, ALU.add).then_inc(g_step, 1)
                        dve.wait_ge(g_step, g + 3)
                        dve.scalar_tensor_tensor(g_e, g_m, -NEG_INF, g_e, ALU.mult, ALU.add).then_inc(g_step, 1)
                        dve.wait_ge(g_step, g + 4)
                        dve.tensor_reduce(g_nmax[:, :], g_e, AX.X, ALU.max, negate=True).then_inc(g_step, 1)
                        for i in range(G):
                            dve.wait_ge(g_transposed, k * G + i + 1)
                            if i >= 2:
                                dve.wait_ge(g_summed, k * G + i - 1)
                            dve.tensor_copy(g_PT[:, i % 2, :], TP[i % 2][:, :]).then_inc(g_pt_ready, 1)
                        h = k * 5
                        dve.wait_ge(g_summed, k * G + G)
                        dve.tensor_scalar(g_rec[:, :], g_den[:, :], DEN_SCALE, None, ALU.mult).then_inc(g_end_step, 1)
                        dve.wait_ge(g_end_step, h + 1)
                        dve.reciprocal(g_rec[:, :], g_rec[:, :]).then_inc(g_end_step, 1)
                        dve.wait_ge(g_end_step, h + 2)
                        dve.scalar_tensor_tensor(g_hp[:, b, :], PA[0][:, 0:D], g_rec[:, :], unscale[:, :], ALU.mult,
                                                 ALU.mult).then_inc(g_end_step, 1)
                        dve.wait_ge(g_end_step, h + 3)
                        dve.tensor_scalar(eneg[:, b, :], g_hp[:, b, :], 0.0, None, ALU.min).then_inc(g_neg_ready, 1)
                        dve.wait_ge(g_neg_ready, k + 1)
                        dve.tensor_scalar(g_hp[:, b, :], g_hp[:, b, :], 0.0, -1.0, ALU.max,
                                          ALU.add).then_inc(g_end_step, 1)
                        dve.wait_ge(g_end_step, h + 4)
                        dve.tensor_tensor(g_hp[:, b, :], g_hp[:, b, :], x_sb[:, s, :].rearrange("p s d -> p (s d)"),
                                          ALU.add).then_inc(g_end_step, 1)
                        dve.wait_ge(g_end_step, h + 5)
                        dve.wait_ge(g_eneg_ready, k + 1)
                        if b == 0 and not first:
                            dve.wait_ge(g_stored, w * 16)
                        dve.tensor_tensor(res[:, b, :], g_hp[:, b, :], eneg[:, b, :],
                                          ALU.add).then_inc(g_res_ready, 1)

                general_group(0, True)
                with dve.Fori(1, G) as w:
                    general_group(w, False)

        @block.scalar
        def _(act):
            act.dma_start(W_sb[:, :], W[:, :]).then_inc(w_loaded, 16)
            act.dma_start(a_sb[:, 0, :], a1.partition_broadcast(P)).then_inc(a_loaded, 16)
            act.dma_start(a_sb[:, 1, :], a2.partition_broadcast(P)).then_inc(a_loaded, 16)

            act.wait_ge(w_loaded, 16)
            act.activation(wsq, W_sb, ACT.Square).then_inc(wsq_ready, 1)
            act.wait_ge(consts_set, 5)
            act.wait_ge(wa_step, 4)
            for a in range(2):
                act.activation(warep[:, a, :], ones[:, :], ACT.Copy,
                               scale=Wext[:, D + a:D + a + 1]).then_inc(wext_ready, 1)

            def store_hT(w):
                act.wait_ge(h_transposed, w + 1)
                act.activation(hT[:, slots(w), :], TP[w % 2][:, :].rearrange("p (s q) -> p s q", s=B), ACT.Relu,
                               accum_out=hsum[:, w:w + 1]).then_inc(hT_ready, 1)

            def signs(w, first, last):
                for s in range(first, last):
                    act.activation(T8[:, (w + 1) % 2, s, :], s1row[:, bass.ds(w * GC, GC)], ACT.Sign,
                                   bias=s12[:, s, 1:2]).then_inc(signs_ready, 1)

            def store_row(w):
                act.wait_ge(row_done, w + 1)
                act.activation(s1row[:, w * GC:(w + 1) * GC], PB[w % 2][:, :], ACT.Copy).then_inc(row_stored[0], 1)

            PER_GROUP, EARLY, PER_Y = 3, 26, 2
            store_hT(0)
            store_row(0)
            store_hT(1)
            act.wait_ge(row_stored[0], 1)
            act.wait_ge(s12_ready, 1)
            signs(0, 0, B)
            for w in range(2, G):
                store_hT(w)
                if w % 2:
                    store_row(w - 1)
                s = B + (w - 2) * PER_GROUP
                act.wait_ge(s12_ready, (s + PER_GROUP - 1) // B + 1)
                signs(0, s, s + PER_GROUP)
            act.wait_ge(s12_ready, (EARLY - 1) // B + 1)
            signs(0, B + (G - 2) * PER_GROUP, EARLY)
            act.wait_ge(exps_in, 2)
            act.activation(F1[:, :], sF[:, :], ACT.Exp).then_inc(exps_ready, 1)
            act.activation(F2[:, :], sF[:, :], ACT.Exp, scale=ALPHA).then_inc(exps_ready, 1)
            act.wait_ge(exps_in, 4)
            act.activation(E[:, :, :], u08[:, :, :], ACT.Exp).then_inc(exps_ready, 1)

            act.wait_ge(exps_ready, 2)
            act.wait_ge(s12_ready, G)
            act.wait_ge(wh_stored, G)
            for w in range(G):
                if w < ACT_YA:
                    act.wait_ge(prodA_ready, w + 1)
                    act.activation(YA[:, slots(w), 0:C], prodA[:, w % 2], ACT.Copy).then_inc(highA_ready, 1)
                else:
                    for s in range(w * B, (w + 1) * B):
                        act.activation(YA[:, s, 0:C], Wh[:, s, :], ACT.Copy,
                                       scale=F1[:, s:s + 1]).then_inc(highA_act_ready, 1)
                if w in POOL_YB:
                    n = POOL_YB.index(w)
                    act.wait_ge(prodB_ready, n + 1)
                    act.activation(YB[:, slots(w), 0:C], prodB[:, n % 2], ACT.Copy).then_inc(highB_ready, 1)
                else:
                    for s in range(w * B, (w + 1) * B):
                        act.activation(YB[:, s, 0:C], Wh[:, s, :], ACT.Copy,
                                       scale=F2[:, s:s + 1]).then_inc(highB_act_ready, 1)
                if EARLY + w * PER_Y < S:
                    signs(0, EARLY + w * PER_Y, min(EARLY + (w + 1) * PER_Y, S))

            act.wait_ge(flag_ready, 1)
            usual = act.value_load(flag[0:1, 0:1], min_val=0, max_val=1)
            with act.If(usual > 0):
                def scale_sums(w, b, first=False, final=False):
                    if not first:
                        act.wait_ge(sums_read, w * B + b - B + 2)
                    if final:
                        act.wait_ge(last_b_summed, 1)
                    else:
                        act.wait_ge(half_summed, 1 + FIRST_ORDER.index((b, H - 1)) if first else w * GH + H * (b + 1))
                    act.activation(partB[:, b, :], PB[b % 2][:, 0:2 * C], ACT.Copy,
                                   scale=E[:, 1, bass.ds(w * B + b, 1)]).then_inc(partB_ready, 1)

                def end_exp(w):
                    act.wait_ge(neg_ready, w + 1)
                    act.activation(eneg, eneg, ACT.Exp).then_inc(eneg_ready, 1)

                def end_exp_last(b):
                    act.wait_ge(last_neg_ready, b + 1)
                    act.activation(eneg[:, b, :], eneg[:, b, :], ACT.Exp).then_inc(last_eneg_ready, 1)

                def next_signs(w, c, first=False):
                    if c == 0 and not first:
                        act.wait_ge(bt_ready, w * GH)
                    signs(w + 1, c * S // B, (c + 1) * S // B)

                def group(w, first):
                    next_signs(w, 0, first)
                    if not first:
                        scale_sums(w - 1, B - 1)
                    for b in range(B - 1):
                        if not first:
                            next_signs(w, b + 1)
                            if b == B - 2:
                                end_exp(w - 1)
                        scale_sums(w, b, first)
                        if first:
                            next_signs(w, b + 1)

                act.wait_ge(wh_done, G)
                act.wait_ge(mean_done, 1)
                act.wait_ge(row_done, G)
                act.wait_ge(row_stored[0], G // 2)
                act.wait_ge(row_stored[1], G // 2)
                group(0, True)
                with act.Fori(1, G - 1) as w:
                    group(w, False)
                scale_sums(G - 2, B - 1)
                for b in range(B):
                    scale_sums(G - 1, b, False, b == B - 1)
                    if b == 0:
                        end_exp(G - 2)
                        end_exp_last(0)
                    else:
                        end_exp_last(b)

            with act.Else():
                with act.Fori(0, G) as w:
                    for b in range(B):
                        k = w * B + b
                        act.wait_ge(g_step, k * 5 + 5)
                        act.activation(g_m, g_e, ACT.Exp, bias=g_nmax[:, :],
                                       accum_out=g_den[:, :]).then_inc(g_p_ready, 1)
                        act.wait_ge(g_neg_ready, k + 1)
                        act.activation(eneg[:, b, :], eneg[:, b, :], ACT.Exp).then_inc(g_eneg_ready, 1)

        @block.tensor
        def _(pe):
            pe.wait_ge(consts_set, 5)
            pe.wait_ge(wsq_ready, 1)
            nc.tensor.matmul(PMISC[:, 0:D], ones[:, :], wsq[:, :], start=True, stop=True).then_inc(ssq_done, 1)
            pe.wait_ge(ident_ready, 1)

            def turn_h(w):
                pe.wait_ge(h_dve_ready, sum(DVE_NORM[:w + 1]))
                if DVE_NORM[w] < B:
                    pe.wait_ge(h_pool_ready, (w + 1) * B - sum(DVE_NORM[:w + 1]))
                if w >= 2:
                    pe.wait_ge(hT_ready, w - 1)
                for b in range(B):
                    t = nc.tensor.transpose(TP[w % 2][:, b * P:(b + 1) * P], h_sb[:, w % 2, b, :], ident[:, :])
                t.then_inc(h_transposed, 1)

            def project(w):
                pe.wait_ge(hT_ready, w + 1)
                pe.wait_ge(wext_ready, 3)
                if w >= 2:
                    pe.wait_ge(wh_stored, w - 1)
                    pe.wait_ge(row_stored[w % 2], w // 2)
                    pe.wait_ge(s12_ready, w - 1)
                if w == 1:
                    pe.wait_ge(scale_step, 1)
                for b in range(B):
                    s = w * B + b
                    t = nc.tensor.matmul(projected(w)[:, b // H, b % H, :], hT[:, s, :], Wext[:, :],
                                         start=True, stop=True)
                t.then_inc(wh_done, 1)
                nc.tensor.matmul(PB[w % 2][:, :], warep[:, 0, :], hT[:, slots(w), :].rearrange("p s q -> p (s q)"),
                                 start=True, stop=True).then_inc(row_done, 1)

            turn_h(0)
            project(0)
            turn_h(1)
            for w in range(1, G):
                if w + 1 < G:
                    turn_h(w + 1)
                project(w)
            pe.wait_ge(mm_step, 2)
            pe.wait_ge(wh_stored, G)
            nc.tensor.transpose(PMISC[0:2, 0:P], mm[:, :], ident[:, :]).then_inc(mm_transposed, 1)
            pe.wait_ge(mm_step, 4)
            nc.tensor.matmul(PMISC[:, 0:2], ones[0:2, :], mmD[:, :], start=True, stop=True).then_inc(mm_spread, 1)
            pe.wait_ge(hsum_step, 2)
            pe.wait_ge(mmB_ready, 1)
            nc.tensor.matmul(PMISC[:, 0:D], hsumrep[:, :], Wext[:, 0:D], start=True, stop=True).then_inc(mean_done, 1)

            pe.wait_ge(flag_ready, 1)
            usual = pe.value_load(flag[0:1, 0:1], min_val=0, max_val=1)
            with pe.If(usual > 0):
                def wait_for_half(w, r):
                    pe.wait_ge(at_ready, w * GH + r + 1)
                    b, hf = part(w, r)
                    if hf == 0 and not (b < 2 and isinstance(w, int) and w == 0):
                        pe.wait_ge(sums_read, w * B + b)
                    pe.sem_inc(half_started, 1)

                def sum_a(r, b, s):
                    return nc.tensor.matmul(PA[b % 2][:, 0:2 * C], fp8_slot(V, r, s % HS), YA[:, s, :],
                                            start=s == 0, stop=s == S - 1)

                def sum_b(r, b, s):
                    return nc.tensor.matmul(PB[b % 2][:, 0:2 * C], fp8_slot(BT, r, s % HS), YB[:, s, :],
                                            start=s == 0, stop=s == S - 1)

                def group(w, first, last):
                    for r in range(GH):
                        b, hf = part(w, r)
                        for j in range(HS):
                            s = hf * HS + j
                            if first and b == 0 and j % B == 0:
                                g = s // B
                                if g < ACT_YA:
                                    pe.wait_ge(ya_ready, g + 1)
                                else:
                                    pe.wait_ge(ya_low_ready, (g - ACT_YA + 1) * B)
                                if g in DVE_YB:
                                    pe.wait_ge(yb_dve_ready, B * (DVE_YB.index(g) + 1))
                                else:
                                    pe.wait_ge(yb_pool_ready, POOL_YB.index(g) + 1)
                            if not (last and r == GH - 1):
                                sum_a(r, b, s)
                            t = sum_b(r, b, s)
                        if last and r == GH - 1:
                            t.then_inc(last_b_summed, 1)
                            for s in range(hf * HS, S):
                                t = sum_a(r, b, s)
                        t.then_inc(half_summed, 1)
                        if not (last and r + 1 == GH):
                            wait_for_half(w + (r + 1) // GH, (r + 1) % GH)

                pe.wait_ge(wh_stored, G)
                pe.wait_ge(row_stored[0], G // 2)
                pe.wait_ge(row_stored[1], G // 2)
                pe.wait_ge(at_ready, 1)
                group(0, True, False)
                with pe.Fori(1, G - 1) as w:
                    group(w, False, False)
                group(G - 1, False, True)
            with pe.Else():
                for w in range(G):
                    pe.wait_ge(row_stored[w % 2], G // 2)
                    if w >= 2:
                        pe.wait_ge(g_row_stored, w - 1)
                    nc.tensor.matmul(PB[w % 2][:, :], warep[:, 1, :], hT[:, slots(w), :].rearrange(
                        "p s q -> p (s q)"), start=True, stop=True).then_inc(g_row_done, 1)

                def general_group(w, first):
                    for b in range(B):
                        k = w * B + b
                        pe.wait_ge(g_p_ready, k + 1)
                        if not first or b:
                            pe.wait_ge(g_pt_ready, k * G)
                            pe.wait_ge(g_end_step, k * 5)

                        def turn(i):
                            if i >= 2:
                                pe.wait_ge(g_pt_ready, k * G + i - 1)
                            cols = g_m[:, i * GC:(i + 1) * GC].rearrange("i (q c) -> i q c", c=B)
                            for j in range(B):
                                t = nc.tensor.transpose(TP[i % 2][:, j * P:(j + 1) * P], cols[:, :, j], ident[:, :])
                            t.then_inc(g_transposed, 1)

                        turn(0)
                        for i in range(G):
                            if i + 1 < G:
                                turn(i + 1)
                            pe.wait_ge(g_pt_ready, k * G + i + 1)
                            for j in range(B):
                                t = nc.tensor.matmul(PA[0][:, 0:D], g_PT[:, i % 2, j * P:(j + 1) * P],
                                                     Wh[:, i * B + j, 0:D], start=(i == 0 and j == 0),
                                                     stop=(i == G - 1 and j == B - 1))
                            t.then_inc(g_summed, 1)

                pe.wait_ge(wh_stored, G)
                general_group(0, True)
                with pe.Fori(1, G) as w:
                    general_group(w, False)


def kernel(x, adj, L0_gnn_W, L0_gnn_a1, L0_gnn_a2):
    import numpy as np
    import concourse.bacc as bacc
    from concourse import mybir
    from concourse.bass_utils import run_bass_kernel_spmd

    nc = bacc.Bacc("TRN2", target_bir_lowering=False, num_devices=1)
    arrays, args = {}, []
    n, p, b = x.shape[0], 128, 4
    adjT = np.asarray(adj).reshape(n // (p * b), p, b, n // (p * b), p, b).transpose(0, 2, 4, 3, 5, 1).reshape(
        n // (p * b), b, p, n)
    for name, a in (("x", x), ("adj", adj), ("adjT", adjT), ("W", L0_gnn_W), ("a1", L0_gnn_a1), ("a2", L0_gnn_a2)):
        a = np.ascontiguousarray(a)
        arrays[f"in_{name}"] = a
        args.append(nc.dram_tensor(f"in_{name}", a.shape, mybir.dt.from_np(a.dtype), kind="ExternalInput").ap())
    out = nc.dram_tensor("out", x.shape, mybir.dt.float32, kind="ExternalOutput").ap()
    build(nc, *args, out)
    r = run_bass_kernel_spmd(nc, [arrays], core_ids=[0])
    return r.results[0]["out"]
```
